# Optimizing a Trainium2 kernel written in Bass

```python
import numpy as np
import jax
import jax.numpy as jnp

def _softmax(x, axis=-1):
    return jax.nn.softmax(x, axis=axis)

def _gelu(x):
    return jax.nn.gelu(x, approximate=True)

def _silu(x):
    return jax.nn.silu(x)

def _sigmoid(x):
    return jax.nn.sigmoid(x)

def _layernorm(x, axis=-1, eps=1e-05):
    m = jnp.mean(x, axis=axis, keepdims=True)
    v = jnp.var(x, axis=axis, keepdims=True)
    return (x - m) / jnp.sqrt(v + eps)

def _scatter_add(tgt, idx, src, axis=0):
    return tgt.at[idx].add(src)

def _segment_sum(src, seg, n):
    return jax.ops.segment_sum(src, seg, n)
kernel_name = 'mk_seq_preln_d1_jaxref_r8_dafdef'

def setup_inputs(seed: int=0):
    np.random.seed(seed)
    _w = jnp.asarray

    def _L0_attn_setup():
        import jax, jax.numpy as jnp
        import numpy as np
        import math
        H = 16
        EPS = 1e-05
        key = jax.random.key(seed)
        ks = jax.random.split(key, 4)
        B, T, D = (2, 256, 128)
        s = 1.0 / math.sqrt(D)
        return {'x': jax.random.normal(ks[0], (B, T, D), dtype=jnp.float32), 'ln_g': jnp.ones((D,), jnp.float32), 'ln_b': jnp.zeros((D,), jnp.float32), 'Wq': jax.random.normal(ks[1], (D, D), jnp.float32) * s, 'bq': jnp.zeros((D,), jnp.float32), 'Wk': jax.random.normal(ks[2], (D, D), jnp.float32) * s, 'bk': jnp.zeros((D,), jnp.float32), 'Wv': jax.random.normal(ks[3], (D, D), jnp.float32) * s, 'bv': jnp.zeros((D,), jnp.float32)}
    _L0_attn_in = _L0_attn_setup()

    def _L0_ffn_setup():
        import jax, jax.numpy as jnp
        import numpy as np
        B, T, C = (2, 128, 128)
        H = 512
        E_R, E_S, K = (8, 2, 2)

        def _rmsnorm(x, g):
            eps = jnp.finfo(x.dtype).eps
            return x * jax.lax.rsqrt(jnp.mean(x * x, axis=-1, keepdims=True) + eps) * g

        def _experts_mlp(x, g, W1, b1, W2, b2):
            xn = _rmsnorm(x, g)
            h = jnp.einsum('btc,ech->bteh', xn, W1) + b1
            h = jax.nn.gelu(h, approximate=False)
            return jnp.einsum('bteh,ehc->btec', h, W2) + b2
        key = jax.random.key(seed)
        ks = jax.random.split(key, 12)
        s = 0.02
        return {'u': jax.random.normal(ks[0], (B, T, C), dtype=jnp.float32), 'g_shared': jnp.ones((C,), jnp.float32), 'W1_s': jax.random.normal(ks[1], (E_S, C, H), jnp.float32) * s, 'b1_s': jax.random.normal(ks[2], (E_S, H), jnp.float32) * s, 'W2_s': jax.random.normal(ks[3], (E_S, H, C), jnp.float32) * s, 'b2_s': jax.random.normal(ks[4], (E_S, C), jnp.float32) * s, 'g_routed': jnp.ones((C,), jnp.float32), 'W1_r': jax.random.normal(ks[5], (E_R, C, H), jnp.float32) * s, 'b1_r': jax.random.normal(ks[6], (E_R, H), jnp.float32) * s, 'W2_r': jax.random.normal(ks[7], (E_R, H, C), jnp.float32) * s, 'b2_r': jax.random.normal(ks[8], (E_R, C), jnp.float32) * s, 'centroids': jax.random.normal(ks[9], (C, E_R), jnp.float32) * s}
    _L0_ffn_in = _L0_ffn_setup()
    _d = {'L0_attn_x': _L0_attn_in['x'], 'L0_attn_ln_g': _L0_attn_in['ln_g'], 'L0_attn_ln_b': _L0_attn_in['ln_b'], 'L0_attn_Wq': _L0_attn_in['Wq'], 'L0_attn_bq': _L0_attn_in['bq'], 'L0_attn_Wk': _L0_attn_in['Wk'], 'L0_attn_bk': _L0_attn_in['bk'], 'L0_attn_Wv': _L0_attn_in['Wv'], 'L0_attn_bv': _L0_attn_in['bv'], 'L0_ffn_g_shared': _L0_ffn_in['g_shared'], 'L0_ffn_W1_s': _L0_ffn_in['W1_s'], 'L0_ffn_b1_s': _L0_ffn_in['b1_s'], 'L0_ffn_W2_s': _L0_ffn_in['W2_s'], 'L0_ffn_b2_s': _L0_ffn_in['b2_s'], 'L0_ffn_g_routed': _L0_ffn_in['g_routed'], 'L0_ffn_W1_r': _L0_ffn_in['W1_r'], 'L0_ffn_b1_r': _L0_ffn_in['b1_r'], 'L0_ffn_W2_r': _L0_ffn_in['W2_r'], 'L0_ffn_b2_r': _L0_ffn_in['b2_r'], 'L0_ffn_centroids': _L0_ffn_in['centroids']}
    _x0 = _d['L0_attn_x']
    _d['L0_attn_x'] = jax.random.normal(jax.random.fold_in(jax.random.key(seed), 1), (4, 1024, 128), dtype=_x0.dtype)
    del _x0
    return _d

def reference(L0_attn_x, L0_attn_ln_g, L0_attn_ln_b, L0_attn_Wq, L0_attn_bq, L0_attn_Wk, L0_attn_bk, L0_attn_Wv, L0_attn_bv, L0_ffn_g_shared, L0_ffn_W1_s, L0_ffn_b1_s, L0_ffn_W2_s, L0_ffn_b2_s, L0_ffn_g_routed, L0_ffn_W1_r, L0_ffn_b1_r, L0_ffn_W2_r, L0_ffn_b2_r, L0_ffn_centroids):

    def _L0_attn_ref(x, ln_g, ln_b, Wq, bq, Wk, bk, Wv, bv):
        import jax, jax.numpy as jnp
        import numpy as np
        import math
        H = 16
        EPS = 1e-05
        B, T, D = x.shape
        mu = jnp.mean(x, axis=-1, keepdims=True)
        var = jnp.mean(jnp.square(x - mu), axis=-1, keepdims=True)
        xn = (x - mu) * jax.lax.rsqrt(var + EPS) * ln_g + ln_b
        q = (xn @ Wq + bq).reshape(B, T, H, D // H)
        k = (xn @ Wk + bk).reshape(B, T, H, D // H)
        v = (xn @ Wv + bv).reshape(B, T, H, D // H)
        scale = 1.0 / math.sqrt(D // H)
        attn = jnp.einsum('bnhd,bmhd->bnmh', q, k) * scale
        w = jax.nn.softmax(attn, axis=2)
        y = jnp.einsum('bnmh,bmhd->bnhd', w, v).reshape(B, T, D)
        return y

    def _L0_ffn_ref(u, g_shared, W1_s, b1_s, W2_s, b2_s, g_routed, W1_r, b1_r, W2_r, b2_r, centroids):
        import jax, jax.numpy as jnp
        import numpy as np
        B, T, C = (2, 128, 128)
        H = 512
        E_R, E_S, K = (8, 2, 2)

        def _rmsnorm(x, g):
            eps = jnp.finfo(x.dtype).eps
            return x * jax.lax.rsqrt(jnp.mean(x * x, axis=-1, keepdims=True) + eps) * g

        def _experts_mlp(x, g, W1, b1, W2, b2):
            xn = _rmsnorm(x, g)
            h = jnp.einsum('btc,ech->bteh', xn, W1) + b1
            h = jax.nn.gelu(h, approximate=False)
            return jnp.einsum('bteh,ehc->btec', h, W2) + b2
        h_s = _experts_mlp(u, g_shared, W1_s, b1_s, W2_s, b2_s).sum(axis=-2)
        scores = jax.nn.sigmoid(u @ centroids)
        gpk, i_topk = jax.lax.top_k(scores, K)
        gk = gpk / scores.sum(axis=-1, keepdims=True)
        routed_all = _experts_mlp(u, g_routed, W1_r, b1_r, W2_r, b2_r)
        routed_topk = jnp.take_along_axis(routed_all, i_topk[..., None], axis=2)
        h_r = (gk[..., None] * routed_topk).sum(axis=-2)
        return u + h_s + h_r
    x = L0_attn_x
    x = x + _L0_attn_ref(_layernorm(x, axis=-1), L0_attn_ln_g, L0_attn_ln_b, L0_attn_Wq, L0_attn_bq, L0_attn_Wk, L0_attn_bk, L0_attn_Wv, L0_attn_bv)
    x = x + _L0_ffn_ref(_layernorm(x, axis=-1), L0_ffn_g_shared, L0_ffn_W1_s, L0_ffn_b1_s, L0_ffn_W2_s, L0_ffn_b2_s, L0_ffn_g_routed, L0_ffn_W1_r, L0_ffn_b1_r, L0_ffn_W2_r, L0_ffn_b2_r, L0_ffn_centroids)
    return x

_drawn_inputs = setup_inputs


def setup_inputs(seed=0):
    import zlib

    import numpy as np

    out = dict(_drawn_inputs(seed))
    spreads = {'L0_attn_ln_g': (1.0, 0.2),
     'L0_attn_ln_b': (0.0, 0.1),
     'L0_attn_bq': (0.0, 0.775),
     'L0_attn_bk': (0.0, 2.0),
     'L0_attn_bv': (0.0, 0.1),
     'L0_ffn_g_shared': (1.0, 0.6),
     'L0_ffn_g_routed': (1.0, 0.6)}
    factors = {'L0_ffn_b1_s': 22.048,
     'L0_ffn_b2_s': 4.134,
     'L0_ffn_W1_r': 8.0,
     'L0_ffn_b1_r': 8.0,
     'L0_ffn_W2_r': 8.0,
     'L0_ffn_b2_r': 26.892,
     'L0_ffn_centroids': 8.0}
    for name, (base, spread) in spreads.items():
        noise = np.random.default_rng([zlib.crc32(name.encode()), seed]).standard_normal(out[name].shape)
        drawn = base * np.exp(spread * noise) if base else spread * noise
        out[name] = jnp.asarray(drawn.astype(out[name].dtype))
    for name, factor in factors.items():
        out[name] = (out[name] * factor).astype(out[name].dtype)
    return out
```

```python
import math
import struct
from contextlib import ExitStack

import concourse.bass as bass
from concourse import mybir

F32 = mybir.dt.float32
F32R = mybir.dt.float32r
BF16 = mybir.dt.bfloat16
ALU = mybir.AluOpType
ACT = mybir.ActivationFunctionType
AX = mybir.AxisListType

P = 128
B, T, D = 4, 1024, 128
H, DH = 16, 8
TILES = T // P
HALF = 512
EPS = 1e-5
EPS_RMS = 1.1920929e-07
SCALE = 1.0 / math.sqrt(DH)

HEADS = B * H
PARTS = 3
STACK = PARTS * PARTS * DH
BIAS = STACK
TWO_ONES = struct.unpack("f", struct.pack("I", 0x3F803F80))[0]
SLOTS = 4
VCOLS = 32
QUARTER = T // 4

E_SHARED, E_ROUTED, TOPK = 2, 8, 2
EXPERTS = E_SHARED + E_ROUTED
HID = 512
HCH = HID // P
GROUP = 512
GROUPS = B * T // GROUP


def after(eng, sem, count):
    if not isinstance(count, int) or count > 0:
        eng.wait_ge(sem, count)


def over_heads(eng, head):
    for u in range(SLOTS):
        head(u, u)
    with eng.Fori(1, HEADS // SLOTS - 1) as quad:
        for u in range(SLOTS):
            head(quad * SLOTS + u, u)
    for u in range(SLOTS):
        head(HEADS - SLOTS + u, u)


def over_groups(eng, step):
    for e in range(EXPERTS):
        step(0, e)
    with eng.Fori(1, GROUPS) as group:
        for e in range(EXPERTS):
            step(group, e)


HALVES = 2 * TILES

RING = [("half", n) for n in range(8)] + [("rows", 0)] + [("half", n) for n in range(8, 12)] + [("turn", 0)] + \
       [("half", n) for n in range(12, 16)]
def exists(g):
    return not isinstance(g, int) or 0 <= g < HEADS


def result(g, place):
    if isinstance(g, int) and g < 0:
        back = (g * len(RING) + place)
        return ("rows", 0, 0) if back == -1 else ("half", 1, HALVES + back + 1) if back >= -HALVES - 1 else \
            ("half", 0, 2 * HALVES + back + 1)
    kind, n = RING[place]
    head = g + {"half": 2, "rows": 1, "turn": -1}[kind]
    return (kind, head, n) if exists(head) else None


def transformer_block(nc, x, ln_g, ln_b, Wq, bq, Wk, bk, Wv, bv, g_shared, W1_s, b1_s, W2_s, b2_s,
                      g_routed, W1_r, b1_r, W2_r, b2_r, centroids, out):
    ctx = ExitStack()
    with ctx:
        top = [nc.sbuf_base + 31 & ~31]

        def sb(name, shape, dt, at=None):
            size = int(np_size(shape[1:])) * (2 if dt == BF16 else 4)
            offset = top[0] if at is None else at
            if at is None:
                top[0] += (size + 31) // 32 * 32
            return nc.alloc_sbuf_tensor_at(name, shape, dt, offset=offset)

        def pb(name, shape=(P, HALF)):
            return ctx.enter_context(nc.psum_tensor(name, list(shape), F32))

        def sem(name):
            return ctx.enter_context(nc.semaphore(name))

        q_scr = nc.dram_tensor("q_scr", (B, H, PARTS, DH, T), BF16, kind="Internal").ap()
        k_scr = nc.dram_tensor("k_scr", (B, H, PARTS, DH, T), BF16, kind="Internal").ap()

        x_res = sb("x_res", [P, B * TILES, D], F32)
        ident = sb("ident", [P, P], F32)
        identb = sb("identb", [P, P], BF16)
        cols = sb("cols", [P, 4], F32)
        base_loop = top[0]
        y_all = sb("y_all", [P, HEADS, TILES, DH], F32)
        v_all = sb("v_all", [P, HEADS, TILES, DH], F32)
        qs = [sb(f"qs{i}", [P, T], BF16) for i in range(SLOTS)]
        ks = [sb(f"ks{i}", [P, T], BF16) for i in range(SLOTS)]
        base_probs = top[0]
        probs = sb("probs", [P, TILES, T], F32)
        vst = [sb(f"vst{i}", [P, TILES, VCOLS], F32) for i in range(2)]
        negmax = [sb(f"negmax{i}", [P, TILES], F32) for i in range(2)]
        halfmax = [sb(f"halfmax{i}", [P, HALVES], F32) for i in range(2)]
        mparts = [sb(f"mparts{i}", [P, PARTS, TILES], BF16) for i in range(2)]
        zeros = sb("zeros", [P, TILES], F32)
        mrest = sb("mrest", [P, TILES], F32)
        mrows = [sb(f"mrows{i}", [PARTS * TILES, P], BF16) for i in range(2)]
        o_sb = sb("o_sb", [P, QUARTER], F32)
        rsum = sb("rsum", [P, 2, 4], F32)

        w1_high = sb("w1_high", [P, EXPERTS, HID], F32R)
        w1_raw = sb("w1_raw", [P, EXPERTS, HID], F32)
        w1_low = sb("w1_low", [P, EXPERTS, HID], F32R, at=top[0] - EXPERTS * HID * 4)
        w2_high = sb("w2_high", [P, EXPERTS, HCH, D], F32R)
        w2_raw = sb("w2_raw", [P, EXPERTS, HCH, D], F32)
        w2_low = sb("w2_low", [P, EXPERTS, HCH, D], F32R, at=top[0] - EXPERTS * HID * 4)
        g_cols = sb("g_cols", [P, 2], F32)
        b_rows = sb("b_rows", [EXPERTS * (HCH + 1), P], F32)
        b_cols = sb("b_cols", [P, EXPERTS * (HCH + 1)], F32)
        b2_shared = sb("b2_shared", [P, 1], F32)
        cent = sb("cent", [P, E_ROUTED], F32)
        before = sb("before", [P, E_ROUTED, E_ROUTED], F32)
        gate_in = sb("gate_in", [P, E_ROUTED, GROUP], F32)
        acc = sb("acc", [P, GROUP], F32)
        gated = sb("gated", [P, GROUP], F32)

        rT_high = sb("rT_high", [P, B * T], F32R, at=base_probs)
        rT_low = sb("rT_low", [P, B * T], F32R, at=base_probs + B * T * 4)
        at = base_loop
        hid = sb("hid", [P, 2, HCH, GROUP], F32, at=at); at += 2 * HID * 16
        hid_high = sb("hid_high", [P, 2, HCH, GROUP], F32R, at=at); at += 2 * HID * 16
        hid_low = sb("hid_low", [P, 2, HCH, GROUP], F32R, at=at); at += 2 * HID * 16
        assert at <= base_probs
        at = base_loop + HEADS * TILES * DH * 4
        r_tok = sb("r_tok", [P, TILES, D], F32, at=at); at += TILES * D * 4
        rT = sb("rT", [P, T], F32, at=at); at += T * 4
        gT = sb("gT", [E_ROUTED, T], F32, at=at); at += T * 4
        stats3 = sb("stats3", [P, TILES, 6], F32, at=at); at += TILES * 6 * 4
        small3 = sb("small3", [P, 12, TILES], F32, at=at); at += 12 * TILES * 4
        route = sb("route", [P, 8, TILES, E_ROUTED], F32, at=at); at += 8 * TILES * E_ROUTED * 4
        pairs = sb("pairs", [P, 3, TILES, E_ROUTED, E_ROUTED], F32, at=at); at += 3 * TILES * E_ROUTED ** 2 * 4
        assert at <= base_probs

        at = base_probs
        wqkv = sb("wqkv", [P, 3, D], F32, at=at); at += 3 * D * 4
        bv_all = sb("bv_all", [P, D], F32, at=at); at += D * 4
        xn = sb("xn", [P, TILES, D], F32, at=at); at += TILES * D * 4
        xnT = sb("xnT", [P, T], F32, at=at); at += T * 4
        proj = sb("proj", [P, 2, HALF], F32, at=at); at += 2 * HALF * 4
        rest = sb("rest", [P, 2, HALF], F32, at=at); at += 2 * HALF * 4
        parts = sb("parts", [P, 2, PARTS, T], BF16, at=at); at += 2 * PARTS * T * 2
        stats = sb("stats", [P, TILES, 6], F32, at=at); at += TILES * 6 * 4
        small = sb("small", [P, 12, TILES], F32, at=at); at += 12 * TILES * 4
        assert at <= base_probs + TILES * T * 4

        gates_scr = nc.dram_tensor("gates_scr", (E_ROUTED, B * T), F32, kind="Internal").ap()

        bank = [pb(f"bank{i}") for i in range(8)]
        s1, s2 = bank[0:3], bank[3:7]
        o_ps = bank[7]
        t_ps = bank[7]

        rows_ps = s1[RING.index(("rows", 0)) % 3][0:PARTS * TILES, 0:P // 2].bitcast(BF16)
        turn_ps = s1[RING.index(("turn", 0)) % 3][:, 0:2 * P]

        def ring_bank(g, n):
            if isinstance(g, int) and g < 2:
                return (g * HALVES + n) % 3
            return RING.index(("half", n)) % 3

        up_ps = [b[:, :] for b in bank[0:4]]
        score_ps = bank[6][:, 0:TILES * E_ROUTED].rearrange("p (t e) -> p t e", e=E_ROUTED)
        y_ps = [b[:, :] for b in bank[4:7]]

        x_in = sem("x_in")
        consts_in = sem("consts_in")
        ident0 = sem("ident0")
        ident_ready = sem("ident_ready")
        pads_ready = sem("pads_ready")
        vst_padded = sem("vst_padded")
        bn_done = sem("bn_done")
        ln_step = sem("ln_step")
        ln_root = sem("ln_root")
        xn_ready = sem("xn_ready")
        xt_full = sem("xt_full")
        xnT_ready = sem("xnT_ready")
        qk_full = sem("qk_full")
        proj_ready = sem("proj_ready")
        part_step = sem("part_step")
        parts_ready = sem("parts_ready")
        v_full = sem("v_full")
        v_ready = sem("v_ready")
        parts_out = [sem(f"parts_out{i}") for i in range(2)]

        qk_in = [sem(f"qk_in{i}") for i in range(SLOTS)]
        bias_in = [sem(f"bias_in{i}") for i in range(SLOTS)]
        s1_full = sem("s1_full")
        half_done = sem("half_done")
        max_done = sem("max_done")
        split_step = sem("split_step")
        split_done = sem("split_done")
        mrows_full = sem("mrows_full")
        mrows_copied = sem("mrows_copied")
        s2_full = sem("s2_full")
        exp_done = sem("exp_done")
        vst_ready = sem("vst_ready")
        pv_done = sem("pv_done")
        o_copied = sem("o_copied")
        t_full = sem("t_full")
        rsum_done = sem("rsum_done")
        norm_done = sem("norm_done")
        w_in = [sem(f"w_in{i}") for i in range(4)]
        ffn_in = sem("ffn_in")
        w_scaled = sem("w_scaled")
        w_high = sem("w_high")
        w_ready = sem("w_ready")
        before_set = sem("before_set")
        before_ready = sem("before_ready")
        bias_turned = sem("bias_turned")
        b_cols_ready = sem("b_cols_ready")
        x1_done = sem("x1_done")
        bn3_done = sem("bn3_done")
        ln3_step = sem("ln3_step")
        ln3_root = sem("ln3_root")
        r_ready = sem("r_ready")
        x_sum_ready = sem("x_sum_ready")
        rt_full = sem("rt_full")
        rT_ready = sem("rT_ready")
        rT_high_ready = sem("rT_high_ready")
        rT_split = sem("rT_split")
        score_full = sem("score_full")
        route_step = sem("route_step")
        score_exp = sem("score_exp")
        gates_ready = sem("gates_ready")
        gt_full = sem("gt_full")
        gT_ready = sem("gT_ready")
        gates_out = sem("gates_out")
        gate_here = [sem(f"gate_here{i}") for i in range(E_ROUTED)]
        up_full = sem("up_full")
        gelu_done = sem("gelu_done")
        high_done = sem("high_done")
        low_done = sem("low_done")
        down_done = sem("down_done")
        y_read = sem("y_read")
        acc_step = sem("acc_step")
        acc_turned = sem("acc_turned")
        group_done = sem("group_done")
        stored = sem("stored")

        block = ctx.enter_context(nc.Block())

        LN_STEPS = 12
        ROUTE_STEPS = 10
        N_CONSTS = 8

        @block.sync
        def _(sp):
            for i, v in enumerate((ln_g, ln_b, bq, bk)):
                sp.dma_start(cols[:, i:i + 1], v.rearrange("(p a) -> p a", a=1)).then_inc(consts_in, 16)
            for i, w in enumerate((Wq, Wk, Wv)):
                sp.dma_start(wqkv[:, i, :], w).then_inc(consts_in, 16)
            sp.dma_start(bv_all[:, :], bv.rearrange("(a n) -> a n", a=1).to_broadcast([P, D])
                         ).then_inc(consts_in, 16)
            x_tiles = x.rearrange("b (t p) d -> b p t d", p=P)
            for b in range(B):
                after(sp, x_in, 16 * b)
                sp.dma_start(x_res[:, b * TILES:(b + 1) * TILES, :], x_tiles[b]).then_inc(x_in, 16)

            for i, (w, lo, n) in enumerate(((W1_s, 0, E_SHARED), (W1_r, E_SHARED, E_ROUTED))):
                sp.dma_start(w1_raw[:, lo:lo + n, :], w.rearrange("e p n -> p e n")).then_inc(w_in[i], 16)
            for i, (w, lo, n) in enumerate(((W2_s, 0, E_SHARED), (W2_r, E_SHARED, E_ROUTED))):
                for e in range(n):
                    sp.dma_start(w2_raw[:, lo + e, :, :], w[e].rearrange("(k p) n -> p k n", p=P)
                                 ).then_inc(w_in[2 + i], 16)
            sp.dma_start(b_rows[0:E_SHARED * HCH, :], b1_s.rearrange("e (k p) -> (e k) p", p=P)).then_inc(ffn_in, 16)
            sp.dma_start(b_rows[E_SHARED * HCH:EXPERTS * HCH, :], b1_r.rearrange("e (k p) -> (e k) p", p=P)
                         ).then_inc(ffn_in, 16)
            sp.dma_start(b_rows[EXPERTS * HCH:EXPERTS * HCH + E_SHARED, :], b2_s).then_inc(ffn_in, 16)
            sp.dma_start(b_rows[EXPERTS * HCH + E_SHARED:, :], b2_r).then_inc(ffn_in, 16)
            sp.dma_start(g_cols[:, 0:1], g_shared.rearrange("(p a) -> p a", a=1)).then_inc(ffn_in, 16)
            sp.dma_start(g_cols[:, 1:2], g_routed.rearrange("(p a) -> p a", a=1)).then_inc(ffn_in, 16)
            sp.dma_start(cent[:, :], centroids).then_inc(ffn_in, 16)

            with sp.Fori(0, B) as b:
                for i, scr in enumerate((q_scr, k_scr)):
                    sp.wait_ge(parts_ready, 4 * b + 2 * i + 2)
                    for part in range(PARTS):
                        sp.dma_start(scr[b, :, part, :, :], parts[:, i, part, :]).then_inc(parts_out[i], 16)
            for i in range(2):
                sp.wait_ge(parts_out[i], 16 * PARTS * B)

            q_heads = q_scr.rearrange("b h i d n -> (b h) i d n")
            k_heads = k_scr.rearrange("b h i d n -> (b h) (i d) n")

            def load(g, u):
                if not exists(g):
                    return
                after(sp, s2_full, HALVES * (g - SLOTS + 1))
                for i in range(PARTS):
                    rows = slice(i * PARTS * DH, (i + 1) * PARTS * DH)
                    src = q_heads[g, i, :, :].unsqueeze(0).to_broadcast([PARTS, DH, T])
                    sp.dma_start(qs[u][rows, :], src).then_inc(qk_in[u], 16)
                src = k_heads[g, :, :].unsqueeze(0).to_broadcast([PARTS, PARTS * DH, T])
                sp.dma_start(ks[u][0:STACK, :], src).then_inc(qk_in[u], 16)

            def bias_rows(g, u):
                if not exists(g):
                    return
                sp.wait_ge(mrows_copied, g + 1)
                sp.dma_start(qs[u][BIAS:BIAS + PARTS, :].rearrange("i (t n) -> i t n", n=P),
                             mrows[u % 2][:, :]).then_inc(bias_in[u], 16)

            sp.wait_ge(pads_ready, 1)
            for g in range(SLOTS - 1):
                load(g, g)
            bias_rows(0, 0)

            def head(g, u):
                load(g + SLOTS - 1, (u + SLOTS - 1) % SLOTS)
                bias_rows(g + 1, (u + 1) % SLOTS)

            over_heads(sp, head)

            with sp.Fori(0, B) as b:
                sp.wait_ge(gT_ready, 2 * b + 2)
                sp.dma_start(gates_scr.rearrange("e (b n) -> b e n", b=B)[b, :, :], gT[:, :]).then_inc(gates_out, 16)
            sp.wait_ge(gates_out, 16 * B)
            gates_by_group = gates_scr.rearrange("e (g n) -> g e n", g=GROUPS)
            out_by_group = out.rearrange("b (g t p) d -> (b g) p t d", p=P, t=GROUP // P)

            def load_gates(group):
                for r in range(E_ROUTED):
                    after(sp, acc_step, E_ROUTED * (group - 1) + r + 1)
                    sp.dma_start(gate_in[:, r, :],
                                 gates_by_group[group, r, :].unsqueeze(0).to_broadcast([P, GROUP])
                                 ).then_inc(gate_here[r], 16)

            load_gates(0)
            with sp.Fori(0, GROUPS - 1) as group:
                load_gates(group + 1)
                sp.wait_ge(group_done, group + 1)
                sp.dma_start(out_by_group[group, :, :, :],
                             x_res[:, :, :].rearrange("p (g t) d -> p g t d", g=GROUPS)[:, group, :, :]
                             ).then_inc(stored, 16)
            sp.wait_ge(group_done, GROUPS)
            sp.dma_start(out_by_group[GROUPS - 1, :, :, :], x_res[:, (GROUPS - 1) * 4:, :]).then_inc(stored, 16)
            sp.wait_ge(stored, 16 * GROUPS)

        @block.gpsimd
        def _(pool):
            nc.gpsimd.memset(ident[:], 0.0).then_inc(ident0, 1)
            nc.gpsimd.memset(identb[:], 0.0).then_inc(ident0, 1)
            pool.wait_ge(ident0, 2)
            for m in (ident, identb):
                nc.gpsimd.affine_select(out=m[:], in_=m[:], compare_op=ALU.not_equal, fill=1.0, base=0,
                                        pattern=[[-1, P]], channel_multiplier=1).then_inc(ident_ready, 1)
            nc.gpsimd.memset(zeros[:], 0.0)
            for i in range(2):
                nc.gpsimd.memset(vst[i][:, :, DH + 1:], 0.0)
                last = nc.gpsimd.memset(vst[i][:, :, DH:DH + 1], 1.0)
            last.then_inc(vst_padded, 1)

            nc.gpsimd.memset(before[:], 1.0).then_inc(before_set, 1)
            pool.wait_ge(before_set, 1)
            nc.gpsimd.affine_select(out=before[:], in_=before[:], compare_op=ALU.is_gt, fill=0.0, base=0,
                                    pattern=[[1, E_ROUTED], [-1, E_ROUTED]], channel_multiplier=0
                                    ).then_inc(before_ready, 1)

            pool.wait_ge(ffn_in, 16 * 7)
            for i, (lo, n) in enumerate(((0, E_SHARED), (E_SHARED, E_ROUTED))):
                raw, high, low = (w[:, lo:lo + n, :] for w in (w1_raw, w1_high, w1_low))
                pool.wait_ge(w_in[i], 16)
                nc.gpsimd.tensor_scalar(raw, raw, g_cols[:, i:i + 1], 1.0, ALU.mult, ALU.mult).then_inc(w_scaled, 1)
                pool.wait_ge(w_scaled, i + 1)
                nc.gpsimd.tensor_copy(high, raw).then_inc(w_high, 1)
                pool.wait_ge(w_high, i + 1)
                nc.gpsimd.tensor_tensor(low, raw, high.bitcast(F32), ALU.subtract).then_inc(w_ready, 1)
            for i, (lo, n) in enumerate(((0, E_SHARED), (E_SHARED, E_ROUTED))):
                raw, high, low = (w[:, lo:lo + n, :, :] for w in (w2_raw, w2_high, w2_low))
                pool.wait_ge(w_in[2 + i], 16 * n)
                nc.gpsimd.tensor_copy(high, raw).then_inc(w_high, 1)
                pool.wait_ge(w_high, i + 3)
                nc.gpsimd.tensor_tensor(low, raw, high.bitcast(F32), ALU.subtract).then_inc(w_ready, 1)

            def stage_v(g, u):
                if not exists(g):
                    return
                after(pool, pv_done, 4 * (g - 1))
                nc.gpsimd.tensor_copy(vst[u % 2][:, :, 0:DH], v_all[:, g, :, :]).then_inc(vst_ready, 1)

            def split_max(g, u):
                if not exists(g):
                    return
                i = u % 2
                pool.wait_ge(max_done, g + 1)
                after(pool, mrows_full, g - 1)
                nc.gpsimd.tensor_tensor(mparts[i][:, 0, :], negmax[i][:], zeros[:], ALU.add).then_inc(split_step, 1)
                pool.wait_ge(split_step, 3 * g + 1)
                nc.gpsimd.tensor_tensor(mrest[:], negmax[i][:], mparts[i][:, 0, :], ALU.subtract
                                        ).then_inc(split_step, 1)
                pool.wait_ge(split_step, 3 * g + 2)
                nc.gpsimd.tensor_tensor(mparts[i][:, 1, :], mrest[:], zeros[:], ALU.add).then_inc(split_step, 1)
                pool.wait_ge(split_step, 3 * g + 3)
                nc.gpsimd.tensor_tensor(mparts[i][:, 2, :], mrest[:], mparts[i][:, 1, :], ALU.subtract
                                        ).then_inc(split_done, 1)

            pool.wait_ge(v_ready, 2 * B)
            pool.wait_ge(vst_padded, 1)
            stage_v(0, 0)
            split_max(0, 0)
            split_max(1, 1)

            def head(g, u):
                stage_v(g + 1, u + 1)
                split_max(g + 2, u)

            over_heads(pool, head)

        @block.scalar
        def _(act):
            def roots(b):
                for i in range(2):
                    act.wait_ge(ln_step, LN_STEPS * b + (4 if i == 0 else 8))
                    nc.scalar.activation(small[:, 8 + i, :], small[:, 6 + i, :], ACT.Sqrt).then_inc(ln_root, 1)

            def evacuate(b):
                for half in range(2):
                    act.wait_ge(xt_full, 2 * b + half + 1)
                    if half == 0:
                        after(act, v_full, 2 * b)
                    nc.scalar.activation(xnT[:, half * HALF:(half + 1) * HALF], bank[half][:, :],
                                         ACT.Identity, bias=cols[:, 1:2], scale=cols[:, 0:1]).then_inc(xnT_ready, 1)
                for n in range(4):
                    act.wait_ge(qk_full, 4 * b + n + 1)
                    after(act, parts_ready, 4 * b + n - 1)
                    nc.scalar.activation(proj[:, n % 2, :], bank[2 + n % 2][:, :], ACT.Identity,
                                         bias=cols[:, 2 + n // 2:3 + n // 2]).then_inc(proj_ready, 1)

            act.wait_ge(consts_in, 16 * N_CONSTS)
            roots(0)
            roots(1)
            evacuate(0)
            with act.Fori(1, B - 1) as b:
                roots(b + 1)
                evacuate(b)
            evacuate(B - 1)

            def copy_o(g):
                if not exists(g):
                    return
                act.wait_ge(pv_done, 4 * (g + 1))
                after(act, t_full, g)
                nc.scalar.copy(o_sb[:], o_ps[:, 0:QUARTER]).then_inc(o_copied, 1)

            def head(g, u):
                for c in range(TILES):
                    if c == 3:
                        copy_o(g - 1)
                    after(act, pv_done, 4 * (g - 1) + c // 2 + 1)
                    for half in range(2):
                        n = 2 * c + half
                        act.wait_ge(s2_full, HALVES * g + n + 1)
                        nc.scalar.activation(probs[:, c, half * HALF:(half + 1) * HALF], s2[n % 4][:, :], ACT.Exp,
                                             scale=SCALE).then_inc(exp_done, 1)

            over_heads(act, head)
            copy_o(HEADS - 1)

            def prepare(b):
                for i in range(2):
                    act.wait_ge(ln3_step, LN_STEPS * b + (4 if i == 0 else 8))
                    nc.scalar.activation(small3[:, 8 + i, :], small3[:, 6 + i, :], ACT.Sqrt).then_inc(ln3_root, 1)
                for half in range(2):
                    cs = slice(half * HALF, (half + 1) * HALF)
                    act.wait_ge(rt_full, 2 * b + half + 1)
                    after(act, rT_split, 2 * b + half - 1)
                    after(act, score_full, b)
                    nc.scalar.copy(rT[:, cs], bank[half][:, :]).then_inc(rT_ready, 1)
                for half in range(2):
                    cs = slice(half * HALF, (half + 1) * HALF)
                    act.wait_ge(rT_ready, 2 * b + half + 1)
                    nc.scalar.copy(rT_high[:, :].rearrange("p (s n) -> p s n", n=HALF)[:, 2 * b + half, :], rT[:, cs]
                                   ).then_inc(rT_high_ready, 1)
                act.wait_ge(route_step, ROUTE_STEPS * b + 1)
                nc.scalar.activation(route[:, 1, :, :], route[:, 0, :, :], ACT.Exp, scale=-1.0).then_inc(score_exp, 1)
                for half in range(2):
                    cs = slice(half * HALF, (half + 1) * HALF)
                    act.wait_ge(gt_full, 2 * b + half + 1)
                    after(act, gates_out, 16 * b)
                    nc.scalar.copy(gT[:, cs], bank[2 + half][0:E_ROUTED, :]).then_inc(gT_ready, 1)

            act.wait_ge(bias_turned, 1)
            nc.scalar.copy(b_cols[:], t_ps[:, 0:EXPERTS * (HCH + 1)]).then_inc(b_cols_ready, 1)
            prepare(0)
            with act.Fori(1, B) as b:
                prepare(b)

            def up(group, e):
                step = group * EXPERTS + e
                for k in range(HCH + 1):
                    if k < HCH:
                        act.wait_ge(up_full, HCH * step + k + 1)
                        after(act, low_done, HCH * (step - 2) + k + 1)
                        nc.scalar.activation(hid[:, e % 2, k, :], up_ps[k][:, :], ACT.Gelu,
                                             bias=b_cols[:, e * HCH + k:e * HCH + k + 1]).then_inc(gelu_done, 1)
                    if k > 0:
                        act.wait_ge(gelu_done, HCH * step + k)
                        if k == 1:
                            after(act, down_done, step - 1)
                        nc.scalar.copy(hid_high[:, e % 2, k - 1, :], hid[:, e % 2, k - 1, :]).then_inc(high_done, 1)

            act.wait_ge(gates_ready, B)
            act.wait_ge(rT_split, 2 * B)
            act.wait_ge(gates_out, 16 * B)
            over_groups(act, up)

        @block.vector
        def _(dve):
            def normalise(b):
                count = [LN_STEPS * b]

                def link(ins):
                    count[0] = count[0] + 1
                    ins.then_inc(ln_step, 1)
                    dve.wait_ge(ln_step, count[0])

                dve.wait_ge(x_in, 16 * (b + 1))
                nc.vector.memset(small[:, 0, 0:1], 0.0)
                for t in range(TILES):
                    last = nc.vector.bn_stats(stats[:, t, :], x_res[:, b * TILES + t, :])
                last.then_inc(bn_done, 1)
                dve.wait_ge(bn_done, b + 1)
                me, m2e, mo, m2o = (stats[:, :, i] for i in (1, 2, 4, 5))
                V = nc.vector
                s = lambda i: small[:, i, :]
                link(V.tensor_tensor(s(0), me, mo, ALU.subtract))
                V.tensor_tensor(s(2), me, mo, ALU.add)
                V.tensor_tensor(s(3), m2e, m2o, ALU.add)
                link(V.scalar_tensor_tensor(s(1), s(0), D / 4.0, s(0), ALU.mult, ALU.mult))
                link(V.tensor_tensor(s(4), s(3), s(1), ALU.add))
                link(V.tensor_scalar(s(6), s(4), 1.0 / D, EPS, ALU.mult, ALU.add))
                dve.wait_ge(ln_root, 2 * b + 1)
                link(V.reciprocal(s(10), s(8)))
                link(V.tensor_tensor(s(0), s(10), s(10), ALU.mult))
                link(V.scalar_tensor_tensor(s(1), s(4), 1.0 / D, s(0), ALU.mult, ALU.mult))
                link(V.tensor_scalar(s(7), s(1), 1.0, EPS, ALU.mult, ALU.add))
                dve.wait_ge(ln_root, 2 * b + 2)
                link(V.reciprocal(s(11), s(9)))
                link(V.tensor_tensor(s(3), s(10), s(11), ALU.mult))
                link(V.scalar_tensor_tensor(s(5), s(2), -0.5, s(3), ALU.mult, ALU.mult))
                link(V.tensor_copy(s(0), s(5)))
                after(dve, xt_full, 2 * b)
                for t in range(TILES):
                    last = V.tensor_scalar(xn[:, t, :], x_res[:, b * TILES + t, :], small[:, 3, t:t + 1],
                                           small[:, 5, t:t + 1], ALU.mult, ALU.add)
                last.then_inc(xn_ready, 1)

            def split(b):
                for n in range(4):
                    i, half = n // 2, n % 2
                    cs = slice(half * HALF, (half + 1) * HALF)
                    dve.wait_ge(proj_ready, 4 * b + n + 1)
                    if half == 0:
                        after(dve, parts_out[i], 16 * PARTS * b)
                    nc.vector.tensor_copy(parts[:, i, 0, cs], proj[:, half, :]).then_inc(part_step, 1)
                    dve.wait_ge(part_step, 12 * b + 3 * n + 1)
                    nc.vector.tensor_tensor(rest[:, half, :], proj[:, half, :], parts[:, i, 0, cs], ALU.subtract
                                            ).then_inc(part_step, 1)
                    dve.wait_ge(part_step, 12 * b + 3 * n + 2)
                    nc.vector.tensor_copy(parts[:, i, 1, cs], rest[:, half, :]).then_inc(part_step, 1)
                    dve.wait_ge(part_step, 12 * b + 3 * n + 3)
                    nc.vector.tensor_tensor(parts[:, i, 2, cs], rest[:, half, :], parts[:, i, 1, cs], ALU.subtract
                                            ).then_inc(parts_ready, 1)
                for half in range(2):
                    dve.wait_ge(v_full, 2 * b + half + 1)
                    for tt in range(4):
                        t = 4 * half + tt
                        last = nc.vector.tensor_tensor(
                            v_all[:, :, t, :].rearrange("p (b h) d -> p b h d", b=B)[:, b, :, :],
                            bank[4 + half][:, tt * P:(tt + 1) * P].rearrange("p (h d) -> p h d", d=DH),
                            bv_all[:, :].rearrange("p (h d) -> p h d", d=DH), ALU.add)
                    last.then_inc(v_ready, 1)

            for u in range(SLOTS):
                nc.vector.memset(qs[u][64:P, :].bitcast(F32), 0.0)
                last = nc.vector.memset(ks[u][64:P, :].bitcast(F32), TWO_ONES)
            last.then_inc(pads_ready, 1)
            dve.wait_ge(consts_in, 16 * N_CONSTS)
            normalise(0)
            normalise(1)
            split(0)
            with dve.Fori(1, B - 1) as b:
                normalise(b + 1)
                split(b)
            split(B - 1)

            def half_max(g, u, n):
                if not exists(g):
                    return
                if n == 0:
                    after(dve, split_done, g - 1)
                dve.wait_ge(s1_full, HALVES * g + n + 1)
                nc.vector.tensor_reduce(halfmax[u % 2][:, n:n + 1], s1[ring_bank(g, n)][:, :], AX.X, ALU.max
                                        ).then_inc(half_done, 1)
                if n == HALVES - 1:
                    dve.wait_ge(half_done, HALVES * (g + 1))
                    nc.vector.tensor_reduce(negmax[u % 2][:, :], halfmax[u % 2][:, :].rearrange("p (t s) -> p t s", s=2),
                                            AX.X, ALU.max, negate=True).then_inc(max_done, 1)

            def copy_rows(g, u):
                if not exists(g):
                    return
                dve.wait_ge(mrows_full, g + 1)
                nc.vector.tensor_copy(mrows[u % 2][:], rows_ps).then_inc(mrows_copied, 1)

            def normalise_out(g):
                if not exists(g):
                    return
                dve.wait_ge(t_full, g + 1)
                o = turn_ps.rearrange("p (s j c) -> p s j c", s=2, j=4)
                nc.vector.reciprocal(rsum[:, :, :].unsqueeze(3), o[:, :, :, DH:DH + 1]).then_inc(rsum_done, 1)
                dve.wait_ge(rsum_done, g + 1)
                nc.vector.tensor_tensor(y_all[:, g, :, :].rearrange("p (j s) d -> p s j d", s=2), o[:, :, :, 0:DH],
                                        rsum[:, :, :].unsqueeze(3).to_broadcast([P, 2, 4, DH]), ALU.mult
                                        ).then_inc(norm_done, 1)

            for g in range(2):
                for n in range(HALVES):
                    half_max(g, g, n)
            copy_rows(0, 0)

            def head(g, u):
                for kind, n in RING:
                    if kind == "half":
                        half_max(g + 2, u, n)
                    elif kind == "rows":
                        copy_rows(g + 1, u + 1)
                    else:
                        normalise_out(g - 1)

            over_heads(dve, head)
            normalise_out(HEADS - 1)

            dve.wait_ge(norm_done, HEADS)
            dve.wait_ge(b_cols_ready, 1)
            b2 = b_cols[:, EXPERTS * HCH:]
            nc.vector.tensor_tensor(b2_shared[:], b2[:, 0:1], b2[:, 1:2], ALU.add)
            x_batches = x_res[:, :, :].rearrange("p (b t) d -> p b t d", b=B)
            y_batches = y_all[:, :, :, :].rearrange("p (b h) t d -> p b t h d", b=B)
            V = nc.vector

            def prepare(b):
                xb = x_batches[:, b, :, :]
                V.tensor_tensor(xb.rearrange("p t (h d) -> p t h d", d=DH), xb.rearrange("p t (h d) -> p t h d", d=DH),
                                y_batches[:, b, :, :, :], ALU.add).then_inc(x1_done, 1)
                dve.wait_ge(x1_done, b + 1)
                nc.vector.memset(small3[:, 0, 0:1], 0.0)
                for t in range(TILES):
                    last = V.bn_stats(stats3[:, t, :], xb[:, t, :])
                last.then_inc(bn3_done, 1)
                dve.wait_ge(bn3_done, b + 1)
                s = lambda i: small3[:, i, :]
                count = [LN_STEPS * b]

                def link(ins):
                    count[0] = count[0] + 1
                    ins.then_inc(ln3_step, 1)
                    dve.wait_ge(ln3_step, count[0])

                me, m2e, mo, m2o = (stats3[:, :, i] for i in (1, 2, 4, 5))
                link(V.tensor_tensor(s(0), me, mo, ALU.subtract))
                V.tensor_tensor(s(2), me, mo, ALU.add)
                V.tensor_tensor(s(3), m2e, m2o, ALU.add)
                link(V.scalar_tensor_tensor(s(1), s(0), D / 4.0, s(0), ALU.mult, ALU.mult))
                link(V.tensor_tensor(s(4), s(3), s(1), ALU.add))
                link(V.tensor_scalar(s(6), s(4), 1.0 / D, EPS, ALU.mult, ALU.add))
                dve.wait_ge(ln3_root, 2 * b + 1)
                link(V.reciprocal(s(10), s(8)))
                link(V.tensor_tensor(s(0), s(10), s(10), ALU.mult))
                link(V.scalar_tensor_tensor(s(1), s(4), 1.0 / D, s(0), ALU.mult, ALU.mult))
                link(V.tensor_scalar(s(7), s(1), 1.0, EPS_RMS, ALU.mult, ALU.add))
                dve.wait_ge(ln3_root, 2 * b + 2)
                link(V.reciprocal(s(11), s(9)))
                link(V.tensor_tensor(s(3), s(10), s(11), ALU.mult))
                V.scalar_tensor_tensor(s(5), s(2), -0.5, s(3), ALU.mult, ALU.mult)
                link(V.scalar_tensor_tensor(s(0), s(2), -0.5, s(10), ALU.mult, ALU.mult))
                link(V.tensor_scalar(s(1), s(10), 1.0, 1.0, ALU.mult, ALU.add))
                after(dve, rt_full, 2 * b)
                for t in range(TILES):
                    last = V.tensor_scalar(r_tok[:, t, :], xb[:, t, :], small3[:, 3, t:t + 1],
                                           small3[:, 5, t:t + 1], ALU.mult, ALU.add)
                last.then_inc(r_ready, 1)
                for t in range(TILES):
                    last = V.tensor_scalar(xb[:, t, :], xb[:, t, :], small3[:, 1, t:t + 1],
                                           small3[:, 0, t:t + 1], ALU.mult, ALU.add)
                last.then_inc(x_sum_ready, 1)
                for half in range(2):
                    dve.wait_ge(rT_high_ready, 2 * b + half + 1)
                    V.tensor_tensor(rT_low[:, :].rearrange("p (s n) -> p s n", n=HALF)[:, 2 * b + half, :],
                                    rT[:, half * HALF:(half + 1) * HALF],
                                    rT_high[:, :].rearrange("p (s n) -> p s n", n=HALF)[:, 2 * b + half, :]
                                    .bitcast(F32), ALU.subtract).then_inc(rT_split, 1)
                steps = [ROUTE_STEPS * b]

                def rlink(ins):
                    steps[0] = steps[0] + 1
                    ins.then_inc(route_step, 1)
                    dve.wait_ge(route_step, steps[0])

                rt = lambda i: route[:, i, :, :]
                dve.wait_ge(score_full, b + 1)
                rlink(V.tensor_tensor(rt(0), score_ps, s(9).unsqueeze(2).to_broadcast([P, TILES, E_ROUTED]), ALU.mult))
                dve.wait_ge(score_exp, b + 1)
                rlink(V.tensor_scalar(rt(2), rt(1), 1.0, 1.0, ALU.mult, ALU.add))
                rlink(V.reciprocal(rt(3), rt(2)))
                whole = [P, TILES, E_ROUTED, E_ROUTED]
                s_e = rt(3).unsqueeze(3).to_broadcast(whole)
                s_j = rt(3).unsqueeze(2).to_broadcast(whole)
                flat = lambda i: pairs[:, i, :, :, :]
                V.tensor_tensor(flat(0), s_j, s_e, ALU.is_gt)
                rlink(V.tensor_tensor(flat(1), s_j, s_e, ALU.is_equal))
                rlink(V.tensor_tensor(flat(2), flat(1), before[:, :, :].unsqueeze(1).to_broadcast(whole), ALU.mult))
                rlink(V.tensor_tensor(flat(1), flat(0), flat(2), ALU.add))
                rlink(V.tensor_reduce(rt(4), flat(1), AX.X, ALU.add))
                rlink(V.scalar_tensor_tensor(rt(5), rt(4), float(TOPK), rt(3), ALU.is_lt, ALU.mult))
                rlink(V.tensor_reduce(route[:, 6, :, 0], rt(3), AX.X, ALU.add))
                rlink(V.reciprocal(route[:, 7, :, 0], route[:, 6, :, 0]))
                after(dve, gt_full, 2 * b)
                V.tensor_tensor(rt(2), rt(5), route[:, 7, :, 0:1].to_broadcast([P, TILES, E_ROUTED]), ALU.mult
                                ).then_inc(gates_ready, 1)

            prepare(0)
            with dve.Fori(1, B) as b:
                prepare(b)

            def low(group, e):
                step = group * EXPERTS + e
                for k in range(HCH):
                    dve.wait_ge(high_done, HCH * step + k + 1)
                    if k == 0:
                        after(dve, down_done, step - 1)
                    V.tensor_tensor(hid_low[:, e % 2, k, :], hid[:, e % 2, k, :], hid_high[:, e % 2, k, :].bitcast(F32),
                                    ALU.subtract).then_inc(low_done, 1)
                    if k == 1:
                        gather(group if e > 0 else group - 1, (e - 1) % EXPERTS)
                if e == 1:
                    finish(group - 1)

            def gather(group, e):
                if isinstance(group, int) and group < 0 or e == 0:
                    return
                result = group * (E_ROUTED + 1) + max(e - E_SHARED + 1, 0)
                bank = max(e - E_SHARED + 1, 0) % 3
                dve.wait_ge(down_done, EXPERTS * group + e + 1)
                if e == 1:
                    after(dve, acc_turned, group)
                    V.tensor_scalar(acc[:], y_ps[bank], b2_shared[:, 0:1], 1.0, ALU.add, ALU.mult
                                    ).then_inc(y_read, 1)
                    dve.wait_ge(y_read, result + 1)
                else:
                    r = e - E_SHARED
                    dve.wait_ge(gate_here[r], 16 * (group + 1))
                    V.scalar_tensor_tensor(gated[:], y_ps[bank], b2[:, e:e + 1], gate_in[:, r, :], ALU.add, ALU.mult
                                           ).then_inc(y_read, 1)
                    dve.wait_ge(y_read, result + 1)
                    V.tensor_tensor(acc[:], acc[:], gated[:], ALU.add).then_inc(acc_step, 1)

            def finish(group):
                if isinstance(group, int) and group < 0:
                    return
                dve.wait_ge(acc_turned, group + 1)
                xg = x_res[:, :, :].rearrange("p (g t) d -> p g (t d)", g=GROUPS)[:, group, :]
                V.tensor_tensor(xg, t_ps[:, :], xg, ALU.add).then_inc(group_done, 1)

            over_groups(dve, low)
            gather(GROUPS - 1, EXPERTS - 1)
            finish(GROUPS - 1)

        @block.tensor
        def _(pe):
            mm = nc.tensor.matmul

            def project(b):
                pe.wait_ge(xn_ready, b + 1)
                after(pe, xnT_ready, 2 * b)
                for half in range(2):
                    for tt in range(4):
                        t = 4 * half + tt
                        last = nc.tensor.transpose(bank[half][:, tt * P:(tt + 1) * P], xn[:, t, :], ident[:])
                    last.then_inc(xt_full, 1)
                for n in range(4):
                    i, half = n // 2, n % 2
                    if n < 2:
                        pe.wait_ge(xnT_ready, 2 * b + half + 1)
                    after(pe, proj_ready, 4 * b + n - 1)
                    mm(bank[2 + half][:, :], wqkv[:, i, :], xnT[:, half * HALF:(half + 1) * HALF],
                       start=True, stop=True).then_inc(qk_full, 1)
                for half in range(2):
                    after(pe, v_ready, 2 * b - 1 + half)
                    for tt in range(4):
                        t = 4 * half + tt
                        last = mm(bank[4 + half][:, tt * P:(tt + 1) * P], xnT[:, t * P:(t + 1) * P], wqkv[:, 2, :],
                                  start=True, stop=True)
                    last.then_inc(v_full, 1)

            pe.wait_ge(ident_ready, 2)
            pe.wait_ge(consts_in, 16 * N_CONSTS)
            project(0)
            with pe.Fori(1, B) as b:
                project(b)

            def bank_free(g, place):
                while True:
                    place -= 3
                    if place < 0 and not (isinstance(g, int) and g <= 0):
                        g, place = g - 1, place + len(RING)
                    last = result(g, place) if place >= 0 else result(-1, place + len(RING))
                    if last is not None:
                        break
                kind, head, n = last
                if kind == "half":
                    pe.wait_ge(half_done, HALVES * head + n + 1)
                elif kind == "rows":
                    pe.wait_ge(mrows_copied, head + 1)
                else:
                    pe.wait_ge(norm_done, head + 1)

            def scores(g, u, n):
                if not exists(g):
                    return
                if n == 0:
                    pe.wait_ge(qk_in[u], 16 * (g - u + SLOTS))
                if not isinstance(g, int) or g >= 2:
                    bank_free(g - 2, RING.index(("half", n)))
                else:
                    after(pe, half_done, HALVES * g + n - 2)
                t, half = n // 2, n % 2
                mm(s1[ring_bank(g, n)][:, :], qs[u][0:STACK, t * P:(t + 1) * P],
                   ks[u][0:STACK, half * HALF:(half + 1) * HALF], start=True, stop=True).then_inc(s1_full, 1)

            def shifted(g, u, n):
                if n == 0:
                    pe.wait_ge(bias_in[u], 4 * (g - u + SLOTS))
                c, half = n // 2, n % 2
                after(pe, exp_done, HALVES * g + n - 3)
                mm(s2[n % 4][:, :], ks[u][:, c * P:(c + 1) * P], qs[u][:, half * HALF:(half + 1) * HALF],
                   start=True, stop=True).then_inc(s2_full, 1)

            def weigh(g, u, k):
                if not exists(g):
                    return
                pe.wait_ge(exp_done, HALVES * g + 4 * k + 4)
                if k == 0:
                    pe.wait_ge(vst_ready, g + 1)
                    after(pe, o_copied, g)
                for c in (2 * k, 2 * k + 1):
                    for j in range(4):
                        last = mm(o_ps[32 * j:32 * j + VCOLS, 0:QUARTER], vst[u % 2][:, c, :],
                                  probs[:, c, j * QUARTER:(j + 1) * QUARTER], start=(c == 0), stop=(c == TILES - 1))
                last.then_inc(pv_done, 1)

            def rows_of_max(g, u):
                if not exists(g):
                    return
                pe.wait_ge(split_done, g + 1)
                if isinstance(g, int) and g == 0:
                    pe.wait_ge(half_done, 2 * HALVES - 2)
                else:
                    bank_free(g - 1, RING.index(("rows", 0)))
                nc.tensor.transpose(rows_ps, mparts[u % 2][:, :, :].rearrange("p i t -> p (i t)"), identb[:]
                                    ).then_inc(mrows_full, 1)

            def turn(g):
                if not exists(g):
                    return
                pe.wait_ge(o_copied, g + 1)
                bank_free(g + 1, RING.index(("turn", 0)))
                for s in range(2):
                    last = nc.tensor.transpose(turn_ps[:, s * P:(s + 1) * P], o_sb[:, s * P:(s + 1) * P], ident[:])
                last.then_inc(t_full, 1)

            pe.wait_ge(proj_ready, 4 * B)
            pe.wait_ge(v_ready, 2 * B)
            for g in range(2):
                for n in range(HALVES):
                    scores(g, g, n)
            rows_of_max(0, 0)

            def head(g, u):
                ahead = (u + 2) % SLOTS
                for k in range(4):
                    for n in range(4 * k, 4 * k + 4):
                        scores(g + 2, ahead, n)
                        shifted(g, u, n)
                    if k == 1:
                        rows_of_max(g + 1, u + 1)
                    if k == 2:
                        turn(g - 1)
                    if k == 0:
                        weigh(g - 1, u + 1, 3)
                    else:
                        weigh(g, u, k - 1)

            over_heads(pe, head)
            weigh(HEADS - 1, HEADS - 1, 3)
            turn(HEADS - 1)

            pe.wait_ge(ffn_in, 16 * 7)
            pe.wait_ge(norm_done, HEADS)
            rows = EXPERTS * (HCH + 1)
            nc.tensor.transpose(t_ps[:, 0:rows], b_rows[:, :], ident[0:rows, 0:rows]).then_inc(bias_turned, 1)
            pe.wait_ge(max_done, HEADS)
            pe.wait_ge(exp_done, HEADS * HALVES)
            pe.wait_ge(b_cols_ready, 1)

            def prepare(b):
                pe.wait_ge(r_ready, b + 1)
                after(pe, rT_ready, 2 * b)
                for half in range(2):
                    for t in range(4 * half, 4 * half + 4):
                        last = nc.tensor.transpose(bank[half][:, t % 4 * P:(t % 4 + 1) * P], r_tok[:, t, :], ident[:])
                    last.then_inc(rt_full, 1)
                pe.wait_ge(rT_ready, 2 * b + 2)
                after(pe, gates_ready, b)
                for t in range(TILES):
                    last = mm(score_ps[:, t, :], rT[:, t * P:(t + 1) * P], cent[:, :], start=True, stop=True)
                last.then_inc(score_full, 1)
                pe.wait_ge(gates_ready, b + 1)
                after(pe, gT_ready, 2 * b)
                for half in range(2):
                    for t in range(4 * half, 4 * half + 4):
                        last = nc.tensor.transpose(bank[2 + half][0:E_ROUTED, t % 4 * P:(t % 4 + 1) * P], route[:, 2, t, :],
                                                   ident[:])
                    last.then_inc(gt_full, 1)

            prepare(0)
            with pe.Fori(1, B) as b:
                prepare(b)

            pe.wait_ge(w_ready, 4)
            pe.wait_ge(rT_split, 2 * B)
            pe.wait_ge(gT_ready, 2 * B)
            rT_high_groups = rT_high[:, :].rearrange("p (g n) -> p g n", g=GROUPS)
            rT_low_groups = rT_low[:, :].rearrange("p (g n) -> p g n", g=GROUPS)

            def step(group, e):
                number = group * EXPERTS + e
                for k in range(HCH):
                    after(pe, gelu_done, HCH * (number - 1) + k + 1)
                    ks_ = slice(k * P, (k + 1) * P)
                    high, low = w1_high[:, e, ks_], w1_low[:, e, ks_]
                    mm(up_ps[k], high, rT_high_groups[:, group, :], start=True, stop=False)
                    mm(up_ps[k], high, rT_low_groups[:, group, :], start=False, stop=False)
                    mm(up_ps[k], low, rT_high_groups[:, group, :], start=False, stop=True).then_inc(up_full, 1)
                if e > 0:
                    down(group, e - 1)
                else:
                    down(group - 1, EXPERTS - 1)
                if e == 1:
                    turn_acc(group - 1)

            def down(group, e):
                if isinstance(group, int) and group < 0:
                    return
                number = group * EXPERTS + e
                index = max(e - E_SHARED + 1, 0)
                result = group * (E_ROUTED + 1) + index
                if e != 1:
                    after(pe, y_read, result - 2)
                for k in range(HCH):
                    pe.wait_ge(low_done, HCH * number + k + 1)
                    high, low = w2_high[:, e, k, :], w2_low[:, e, k, :]
                    first, final = k == 0 and e != 1, k == HCH - 1 and e != 0
                    mm(y_ps[index % 3], high, hid_high[:, e % 2, k, :], start=first, stop=False)
                    mm(y_ps[index % 3], high, hid_low[:, e % 2, k, :], start=False, stop=False)
                    last = mm(y_ps[index % 3], low, hid_high[:, e % 2, k, :], start=False, stop=final)
                last.then_inc(down_done, 1)

            def turn_acc(group):
                if isinstance(group, int) and group < 0:
                    return
                pe.wait_ge(acc_step, E_ROUTED * (group + 1))
                after(pe, group_done, group)
                for t in range(4):
                    last = nc.tensor.transpose(t_ps[:, t * P:(t + 1) * P], acc[:, t * P:(t + 1) * P], ident[:])
                last.then_inc(acc_turned, 1)

            over_groups(pe, step)
            down(GROUPS - 1, EXPERTS - 1)
            turn_acc(GROUPS - 1)


def np_size(shape):
    n = 1
    for s in shape:
        n *= s
    return n


_INS = ['L0_attn_x', 'L0_attn_ln_g', 'L0_attn_ln_b', 'L0_attn_Wq', 'L0_attn_bq', 'L0_attn_Wk', 'L0_attn_bk',
        'L0_attn_Wv', 'L0_attn_bv', 'L0_ffn_g_shared', 'L0_ffn_W1_s', 'L0_ffn_b1_s', 'L0_ffn_W2_s', 'L0_ffn_b2_s',
        'L0_ffn_g_routed', 'L0_ffn_W1_r', 'L0_ffn_b1_r', 'L0_ffn_W2_r', 'L0_ffn_b2_r', 'L0_ffn_centroids']


def kernel(**inputs):
    import numpy as _np
    import concourse.bacc as _bacc
    from concourse import mybir as _mybir
    from concourse.bass_utils import run_bass_kernel_spmd as _run

    nc = _bacc.Bacc("TRN2", target_bir_lowering=False, num_devices=1)
    arrays, args = {}, []
    for name in _INS:
        a = _np.ascontiguousarray(inputs[name])
        arrays[f"in_{name}"] = a
        args.append(nc.dram_tensor(f"in_{name}", a.shape, _mybir.dt.from_np(a.dtype), kind="ExternalInput").ap())
    args.append(nc.dram_tensor("out_x", (B, T, D), F32, kind="ExternalOutput").ap())
    transformer_block(nc, *args)
    r = _run(nc, [arrays], core_ids=[0])
    return r.results[0]["out_x"]
```

```python
import math
import struct
from contextlib import ExitStack

import concourse.bass as bass
from concourse import mybir

F32 = mybir.dt.float32
F32R = mybir.dt.float32r
BF16 = mybir.dt.bfloat16
ALU = mybir.AluOpType
ACT = mybir.ActivationFunctionType
AX = mybir.AxisListType

P = 128
B, T, D = 4, 1024, 128
H, DH = 16, 8
TILES = T // P
HALF = 512
EPS = 1e-5
EPS_RMS = 1.1920929e-07
SCALE = 1.0 / math.sqrt(DH)

HEADS = B * H
PARTS = 3
STACK = PARTS * PARTS * DH
BIAS = STACK
TWO_ONES = struct.unpack("f", struct.pack("I", 0x3F803F80))[0]
SLOTS = 4
LAG = 2
VCOLS = 32
QUARTER = T // 4

E_SHARED, E_ROUTED, TOPK = 2, 8, 2
EXPERTS = E_SHARED + E_ROUTED
HID = 512
HCH = HID // P
GROUP = 512
GROUPS = B * T // GROUP
GTILES = GROUP // P


def after(eng, sem, count):
    if not isinstance(count, int) or count > 0:
        eng.wait_ge(sem, count)


def over_heads(eng, head):
    for u in range(SLOTS):
        head(u, u)
    with eng.Fori(1, HEADS // SLOTS - 1) as quad:
        for u in range(SLOTS):
            head(quad * SLOTS + u, u)
    for u in range(SLOTS):
        head(HEADS - SLOTS + u, u)


def over_groups(eng, step):
    for e in range(EXPERTS):
        step(0, e)
    with eng.Fori(1, GROUPS - 1) as group:
        for e in range(EXPERTS):
            step(group, e)
    for e in range(EXPERTS):
        step(GROUPS - 1, e)


def has_next(group):
    return not isinstance(group, int) or group < GROUPS - 1


def is_first(group):
    return isinstance(group, int) and group == 0


HALVES = 2 * TILES

RING = [("half", n) for n in range(8)] + [("rows", 0)] + [("half", n) for n in range(8, 12)] + [("turn", 0)] + \
       [("half", n) for n in range(12, 16)]
def exists(g):
    return not isinstance(g, int) or 0 <= g < HEADS


def result(g, place):
    if isinstance(g, int) and g < 0:
        back = (g * len(RING) + place)
        return ("rows", 0, 0) if back == -1 else ("half", 1, HALVES + back + 1) if back >= -HALVES - 1 else \
            ("half", 0, 2 * HALVES + back + 1)
    kind, n = RING[place]
    head = g + {"half": 2, "rows": 1, "turn": -1}[kind]
    return (kind, head, n) if exists(head) else None


def transformer_block(nc, x, ln_g, ln_b, Wq, bq, Wk, bk, Wv, bv, g_shared, W1_s, b1_s, W2_s, b2_s,
                      g_routed, W1_r, b1_r, W2_r, b2_r, centroids, out):
    ctx = ExitStack()
    with ctx:
        top = [nc.sbuf_base + 31 & ~31]

        def sb(name, shape, dt, at=None):
            size = int(np_size(shape[1:])) * (2 if dt == BF16 else 4)
            offset = top[0] if at is None else at
            if at is None:
                top[0] += (size + 31) // 32 * 32
            return nc.alloc_sbuf_tensor_at(name, shape, dt, offset=offset)

        def pb(name, shape=(P, HALF)):
            return ctx.enter_context(nc.psum_tensor(name, list(shape), F32))

        def sem(name):
            return ctx.enter_context(nc.semaphore(name))

        q_scr = nc.dram_tensor("q_scr", (B, H, PARTS, DH, T), BF16, kind="Internal").ap()
        k_scr = nc.dram_tensor("k_scr", (B, H, PARTS, DH, T), BF16, kind="Internal").ap()

        x_res = sb("x_res", [P, B * TILES, D], F32)
        ident = sb("ident", [P, P], F32)
        identb = sb("identb", [P, P], BF16)
        cols = sb("cols", [P, 4], F32)
        base_loop = top[0]
        y_all = sb("y_all", [P, HEADS, TILES, DH], F32)
        v_all = sb("v_all", [P, HEADS, TILES, DH], F32)
        qs = [sb(f"qs{i}", [P, T], BF16) for i in range(SLOTS)]
        ks = [sb(f"ks{i}", [P, T], BF16) for i in range(SLOTS)]
        base_probs = top[0]
        probs = sb("probs", [P, TILES, T], F32)
        vst = [sb(f"vst{i}", [P, TILES, VCOLS], F32) for i in range(2)]
        negmax = [sb(f"negmax{i}", [P, TILES], F32) for i in range(2)]
        halfmax = [sb(f"halfmax{i}", [P, HALVES], F32) for i in range(2)]
        mparts = [sb(f"mparts{i}", [P, PARTS, TILES], BF16) for i in range(2)]
        zeros = sb("zeros", [P, TILES], F32)
        mrest = sb("mrest", [P, TILES], F32)
        mrows = [sb(f"mrows{i}", [PARTS * TILES, P], BF16) for i in range(2)]
        o_sb = sb("o_sb", [P, QUARTER], F32)
        rsum = sb("rsum", [P, 2, 4], F32)

        w1_high = sb("w1_high", [P, EXPERTS, HID], F32R)
        w1_raw = sb("w1_raw", [P, EXPERTS, HID], F32)
        w1_low = sb("w1_low", [P, EXPERTS, HID], F32R, at=top[0] - EXPERTS * HID * 4)
        w2_high = sb("w2_high", [P, EXPERTS, HCH, D], F32R)
        w2_raw = sb("w2_raw", [P, EXPERTS, HCH, D], F32)
        w2_low = sb("w2_low", [P, EXPERTS, HCH, D], F32R, at=top[0] - EXPERTS * HID * 4)
        g_cols = sb("g_cols", [P, 2], F32)
        b_rows = sb("b_rows", [EXPERTS * (HCH + 1), P], F32)
        b_cols = sb("b_cols", [P, EXPERTS * (HCH + 1)], F32)
        b2_shared = sb("b2_shared", [P, 1], F32)
        cent = sb("cent", [P, E_ROUTED], F32)
        before = sb("before", [P, E_ROUTED, E_ROUTED], F32)
        gates_at = top[0]
        gate_in = sb("gate_in", [P, E_ROUTED, GROUP], F32)
        acc = sb("acc", [P, GROUP], F32)
        gated = sb("gated", [P, GROUP], F32)
        stats = sb("stats", [P, B * TILES, 6], F32)
        small = sb("small", [P, 12, B * TILES], F32)

        rT_high = sb("rT_high", [P, B * T], F32R, at=base_probs)
        rT_low = sb("rT_low", [P, B * T], F32R, at=base_probs + B * T * 4)
        at = base_loop
        hid = sb("hid", [P, 2, HCH, GROUP], F32, at=at)
        hid_low = sb("hid_low", [P, 2, HCH, GROUP], F32R, at=at); at += 2 * HID * 16
        hid_high = sb("hid_high", [P, 2, HCH, GROUP], F32R, at=at); at += 2 * HID * 16
        r_tok = sb("r_tok", [P, GTILES, D], F32, at=at); at += GTILES * D * 4
        rT = sb("rT", [P, GROUP], F32, at=at); at += GROUP * 4
        gT = sb("gT", [E_ROUTED, GROUP], F32, at=at); at += GROUP * 4
        route = sb("route", [P, 8, GTILES, E_ROUTED], F32, at=at); at += 8 * GTILES * E_ROUTED * 4
        pairs = sb("pairs", [P, 3, GTILES, E_ROUTED, E_ROUTED], F32, at=at); at += 3 * GTILES * E_ROUTED ** 2 * 4
        assert at <= base_probs

        at = base_probs
        wqkv = sb("wqkv", [P, 3, D], F32, at=at); at += 3 * D * 4
        bv_all = sb("bv_all", [P, D], F32, at=at); at += D * 4
        xn = sb("xn", [P, 2, TILES, D], F32, at=at); at += 2 * TILES * D * 4
        rest = sb("rest", [P, 2, HALF], F32, at=at); at += 2 * HALF * 4
        part_size = PARTS * T * 2
        xnT = sb("xnT", [P, 2, T], F32, at=gates_at)
        parts = [[sb(f"parts{j}{i}", [P, PARTS, T], BF16, at=at + (2 * j + i) * part_size if (j, i) != (1, 1) else
                     gates_at + 2 * T * 4) for i in range(2)] for j in range(2)]
        assert at + 3 * part_size <= base_probs + TILES * T * 4

        gates_scr = nc.dram_tensor("gates_scr", (E_ROUTED, B * T), F32, kind="Internal").ap()

        bank = [pb(f"bank{i}") for i in range(8)]
        s1, s2 = bank[0:3], bank[3:7]
        qk_ps = [bank[i][:, :] for i in (2, 3, 6, 7)]
        o_ps = bank[7]
        t_ps = bank[7]

        rows_ps = s1[RING.index(("rows", 0)) % 3][0:PARTS * TILES, 0:P // 2].bitcast(BF16)
        turn_ps = s1[RING.index(("turn", 0)) % 3][:, 0:2 * P]

        def ring_bank(g, n):
            if isinstance(g, int) and g < 2:
                return (g * HALVES + n) % 3
            return RING.index(("half", n)) % 3

        up_ps = [b[:, :] for b in bank[0:4]]
        score_ps = t_ps[:, 0:GTILES * E_ROUTED].rearrange("p (t e) -> p t e", e=E_ROUTED)
        y_ps = [b[:, :] for b in bank[4:7]]

        x_in = [sem(f"x_in{b}") for b in range(B)]
        consts_in = sem("consts_in")
        ident0 = sem("ident0")
        ident_ready = sem("ident_ready")
        pads_ready = sem("pads_ready")
        vst_padded = sem("vst_padded")
        warm = sem("warm")
        bn_done = sem("bn_done")
        ln_step = sem("ln_step")
        ln_root = sem("ln_root")
        xn_dve = sem("xn_dve")
        xn_act = sem("xn_act")
        xt_full = sem("xt_full")
        xnT_ready = sem("xnT_ready")
        qk_full = sem("qk_full")
        part0_done = sem("part0_done")
        rest_done = sem("rest_done")
        part1_done = sem("part1_done")
        parts_ready = sem("parts_ready")
        v_full = sem("v_full")
        v_ready = sem("v_ready")
        parts_out = [[sem(f"parts_out{j}{i}") for i in range(2)] for j in range(2)]

        qk_in = [sem(f"qk_in{i}") for i in range(SLOTS)]
        bias_in = [sem(f"bias_in{i}") for i in range(SLOTS)]
        s1_full = sem("s1_full")
        half_done = sem("half_done")
        max_done = sem("max_done")
        split_step = sem("split_step")
        split_done = sem("split_done")
        mrows_full = sem("mrows_full")
        mrows_copied = sem("mrows_copied")
        s2_full = sem("s2_full")
        exp_done = sem("exp_done")
        vst_ready = sem("vst_ready")
        pv_done = sem("pv_done")
        o_copied = sem("o_copied")
        t_full = sem("t_full")
        rsum_done = sem("rsum_done")
        norm_done = sem("norm_done")
        w_in = [sem(f"w_in{i}") for i in range(4)]
        ffn_in = sem("ffn_in")
        w_scaled = sem("w_scaled")
        w_high = sem("w_high")
        w_ready = sem("w_ready")
        before_set = sem("before_set")
        before_ready = sem("before_ready")
        bias_turned = sem("bias_turned")
        b_cols_ready = sem("b_cols_ready")
        x1_done = sem("x1_done")
        bn3_done = sem("bn3_done")
        ln3_step = sem("ln3_step")
        ln3_root = sem("ln3_root")
        r_ready = sem("r_ready")
        scale_step = sem("scale_step")
        x_sum_ready = sem("x_sum_ready")
        rt_full = sem("rt_full")
        rT_ready = sem("rT_ready")
        rT_high_ready = sem("rT_high_ready")
        rT_split = sem("rT_split")
        score_full = sem("score_full")
        route_step = sem("route_step")
        score_exp = sem("score_exp")
        gates_ready = sem("gates_ready")
        gt_full = sem("gt_full")
        gT_ready = sem("gT_ready")
        gates_out = sem("gates_out")
        gate_here = [sem(f"gate_here{i}") for i in range(E_ROUTED)]
        up_full = sem("up_full")
        gelu_done = sem("gelu_done")
        high_done = sem("high_done")
        low_done = sem("low_done")
        down_done = sem("down_done")
        y_read = sem("y_read")
        acc_step = sem("acc_step")
        acc_turned = sem("acc_turned")
        group_done = sem("group_done")
        stored = sem("stored")

        block = ctx.enter_context(nc.Block())

        LN_STEPS = 11
        ROUTE_STEPS = 10
        N_CONSTS = 8

        @block.sync
        def _(sp):
            x_tiles = x.rearrange("b (t p) d -> b p t d", p=P)
            sp.dma_start(x_res[:, 0:TILES, :], x_tiles[0]).then_inc(x_in[0], 16)
            for i, v in enumerate((ln_g, ln_b, bq, bk)):
                sp.dma_start(cols[:, i:i + 1], v.rearrange("(p a) -> p a", a=1)).then_inc(consts_in, 16)
            for i, w in enumerate((Wq, Wk, Wv)):
                sp.dma_start(wqkv[:, i, :], w).then_inc(consts_in, 16)
            sp.dma_start(bv_all[:, :], bv.rearrange("(a n) -> a n", a=1).to_broadcast([P, D])
                         ).then_inc(consts_in, 16)
            for b in range(1, B):
                sp.dma_start(x_res[:, b * TILES:(b + 1) * TILES, :], x_tiles[b]).then_inc(x_in[b], 16)

            sp.dma_start(b_rows[0:E_SHARED * HCH, :], b1_s.rearrange("e (k p) -> (e k) p", p=P)).then_inc(ffn_in, 16)
            sp.dma_start(b_rows[E_SHARED * HCH:EXPERTS * HCH, :], b1_r.rearrange("e (k p) -> (e k) p", p=P)
                         ).then_inc(ffn_in, 16)
            sp.dma_start(b_rows[EXPERTS * HCH:EXPERTS * HCH + E_SHARED, :], b2_s).then_inc(ffn_in, 16)
            sp.dma_start(b_rows[EXPERTS * HCH + E_SHARED:, :], b2_r).then_inc(ffn_in, 16)
            sp.dma_start(g_cols[:, 0:1], g_shared.rearrange("(p a) -> p a", a=1)).then_inc(ffn_in, 16)
            sp.dma_start(g_cols[:, 1:2], g_routed.rearrange("(p a) -> p a", a=1)).then_inc(ffn_in, 16)
            sp.dma_start(cent[:, :], centroids).then_inc(ffn_in, 16)
            for i, (w, lo, n) in enumerate(((W1_s, 0, E_SHARED), (W1_r, E_SHARED, E_ROUTED))):
                sp.dma_start(w1_raw[:, lo:lo + n, :], w.rearrange("e p n -> p e n")).then_inc(w_in[i], 16)
            for i, (w, lo, n) in enumerate(((W2_s, 0, E_SHARED), (W2_r, E_SHARED, E_ROUTED))):
                for e in range(n):
                    sp.dma_start(w2_raw[:, lo + e, :, :], w[e].rearrange("(k p) n -> p k n", p=P)
                                 ).then_inc(w_in[2 + i], 16)

            def store_parts(b):
                for i, scr in enumerate((q_scr, k_scr)):
                    sp.wait_ge(parts_ready, 4 * b + 2 * i + 2)
                    for part in range(PARTS):
                        sp.dma_start(scr[b, :, part, :, :], parts[b % 2][i][:, part, :]).then_inc(parts_out[b % 2][i], 16)

            q_heads = q_scr.rearrange("b h i d n -> (b h) i d n")
            k_heads = k_scr.rearrange("b h i d n -> (b h) (i d) n")

            def load(g, u):
                if not exists(g):
                    return
                after(sp, s2_full, HALVES * (g - SLOTS + 1))
                for i in range(PARTS):
                    rows = slice(i * PARTS * DH, (i + 1) * PARTS * DH)
                    src = q_heads[g, i, :, :].unsqueeze(0).to_broadcast([PARTS, DH, T])
                    sp.dma_start(qs[u][rows, :], src).then_inc(qk_in[u], 16)
                src = k_heads[g, :, :].unsqueeze(0).to_broadcast([PARTS, PARTS * DH, T])
                sp.dma_start(ks[u][0:STACK, :], src).then_inc(qk_in[u], 16)

            def bias_rows(g, u):
                if not exists(g):
                    return
                sp.wait_ge(mrows_copied, g + 1)
                sp.dma_start(qs[u][BIAS:BIAS + PARTS, :].rearrange("i (t n) -> i t n", n=P),
                             mrows[u % 2][:, :]).then_inc(bias_in[u], 16)

            store_parts(0)
            sp.wait_ge(pads_ready, 1)
            for i in range(2):
                sp.wait_ge(parts_out[0][i], 16 * PARTS)
            for g in range(SLOTS - 1):
                load(g, g)
            for b in range(1, B):
                store_parts(b)
            for i in range(2):
                sp.wait_ge(parts_out[0][i], 16 * PARTS * (B // 2))
                sp.wait_ge(parts_out[1][i], 16 * PARTS * (B // 2))
            bias_rows(0, 0)

            def head(g, u):
                load(g + SLOTS - 1, (u + SLOTS - 1) % SLOTS)
                bias_rows(g + 1, (u + 1) % SLOTS)

            over_heads(sp, head)

            gates_by_group = gates_scr.rearrange("e (g n) -> g e n", g=GROUPS)
            out_by_group = out.rearrange("b (g t p) d -> (b g) p t d", p=P, t=GTILES)

            def spread_gates(group):
                sp.wait_ge(gT_ready, group + 1)
                sp.dma_start(gates_by_group[group, :, :], gT[:, :]).then_inc(gates_out, 16)
                sp.wait_ge(gates_out, 16 * (group + 1))
                for r in range(E_ROUTED):
                    after(sp, acc_step, E_ROUTED * (group - 1) + r + 1)
                    sp.dma_start(gate_in[:, r, :],
                                 gates_by_group[group, r, :].unsqueeze(0).to_broadcast([P, GROUP])
                                 ).then_inc(gate_here[r], 16)

            spread_gates(0)
            with sp.Fori(0, GROUPS - 1) as group:
                spread_gates(group + 1)
                sp.wait_ge(group_done, group + 1)
                sp.dma_start(out_by_group[group, :, :, :],
                             x_res[:, :, :].rearrange("p (g t) d -> p g t d", g=GROUPS)[:, group, :, :]
                             ).then_inc(stored, 16)
            sp.wait_ge(group_done, GROUPS)
            sp.dma_start(out_by_group[GROUPS - 1, :, :, :], x_res[:, (GROUPS - 1) * GTILES:, :]).then_inc(stored, 16)
            sp.wait_ge(stored, 16 * GROUPS)

        @block.gpsimd
        def _(pool):
            nc.gpsimd.memset(ident[:], 0.0).then_inc(ident0, 1)
            nc.gpsimd.memset(identb[:], 0.0).then_inc(ident0, 1)
            pool.wait_ge(ident0, 2)
            for m in (ident, identb):
                nc.gpsimd.affine_select(out=m[:], in_=m[:], compare_op=ALU.not_equal, fill=1.0, base=0,
                                        pattern=[[-1, P]], channel_multiplier=1).then_inc(ident_ready, 1)
            nc.gpsimd.memset(zeros[:], 0.0).then_inc(warm, 1)
            for i in range(2):
                nc.gpsimd.memset(vst[i][:, :, DH + 1:], 0.0)
                last = nc.gpsimd.memset(vst[i][:, :, DH:DH + 1], 1.0)
            last.then_inc(vst_padded, 1)
            for u in range(SLOTS):
                nc.gpsimd.memset(qs[u][:, :].bitcast(F32), 0.0)
                last = nc.gpsimd.memset(ks[u][:, :].bitcast(F32), TWO_ONES)
            last.then_inc(pads_ready, 1)

            nc.gpsimd.memset(before[:], 1.0).then_inc(before_set, 1)
            pool.wait_ge(before_set, 1)
            nc.gpsimd.affine_select(out=before[:], in_=before[:], compare_op=ALU.is_gt, fill=0.0, base=0,
                                    pattern=[[1, E_ROUTED], [-1, E_ROUTED]], channel_multiplier=0
                                    ).then_inc(before_ready, 1)

            pool.wait_ge(ffn_in, 16 * 7)
            for i, (lo, n) in enumerate(((0, E_SHARED), (E_SHARED, E_ROUTED))):
                raw, high, low = (w[:, lo:lo + n, :] for w in (w1_raw, w1_high, w1_low))
                pool.wait_ge(w_in[i], 16)
                nc.gpsimd.tensor_scalar(high, raw, g_cols[:, i:i + 1], 1.0, ALU.mult, ALU.mult).then_inc(w_high, 1)
                pool.wait_ge(w_high, i + 1)
                nc.gpsimd.tensor_scalar(raw, raw, g_cols[:, i:i + 1], 1.0, ALU.mult, ALU.mult).then_inc(w_scaled, 1)
                pool.wait_ge(w_scaled, i + 1)
                nc.gpsimd.tensor_tensor(low, raw, high.bitcast(F32), ALU.subtract).then_inc(w_ready, 1)
            for i, (lo, n) in enumerate(((0, E_SHARED), (E_SHARED, E_ROUTED))):
                raw, high, low = (w[:, lo:lo + n, :, :] for w in (w2_raw, w2_high, w2_low))
                pool.wait_ge(w_in[2 + i], 16 * n)
                nc.gpsimd.tensor_scalar(high, raw, 1.0, 1.0, ALU.mult, ALU.mult).then_inc(w_high, 1)
                pool.wait_ge(w_high, i + 3)
                nc.gpsimd.tensor_tensor(low, raw, high.bitcast(F32), ALU.subtract).then_inc(w_ready, 1)

            def stage_v(g, u):
                if not exists(g):
                    return
                after(pool, pv_done, 4 * (g - 1))
                nc.gpsimd.tensor_copy(vst[u % 2][:, :, 0:DH], v_all[:, g, :, :]).then_inc(vst_ready, 1)

            def split_max(g, u):
                if not exists(g):
                    return
                i = u % 2
                pool.wait_ge(max_done, g + 1)
                after(pool, mrows_full, g - 1)
                nc.gpsimd.tensor_tensor(mparts[i][:, 0, :], negmax[i][:], zeros[:], ALU.add).then_inc(split_step, 1)
                pool.wait_ge(split_step, 3 * g + 1)
                nc.gpsimd.tensor_tensor(mrest[:], negmax[i][:], mparts[i][:, 0, :], ALU.subtract
                                        ).then_inc(split_step, 1)
                pool.wait_ge(split_step, 3 * g + 2)
                nc.gpsimd.tensor_tensor(mparts[i][:, 1, :], mrest[:], zeros[:], ALU.add).then_inc(split_step, 1)
                pool.wait_ge(split_step, 3 * g + 3)
                nc.gpsimd.tensor_tensor(mparts[i][:, 2, :], mrest[:], mparts[i][:, 1, :], ALU.subtract
                                        ).then_inc(split_done, 1)

            pool.wait_ge(v_ready, 2 * B)
            pool.wait_ge(vst_padded, 1)
            stage_v(0, 0)
            split_max(0, 0)
            split_max(1, 1)

            def head(g, u):
                stage_v(g + 1, u + 1)
                split_max(g + 2, u)

            over_heads(pool, head)

            def add_result(group, e):
                if e < E_SHARED:
                    return
                pool.wait_ge(y_read, group * (E_ROUTED + 1) + e - E_SHARED + 2)
                nc.gpsimd.tensor_tensor(acc[:], acc[:], gated[:], ALU.add).then_inc(acc_step, 1)

            over_groups(pool, add_result)

        @block.scalar
        def _(act):
            def roots(part, i):
                tiles = (slice(0, TILES), slice(TILES, B * TILES))[part]
                act.wait_ge(ln_step, LN_STEPS * part + 4 * i + 4)
                nc.scalar.activation(small[:, 8 + i, tiles], small[:, 6 + i, tiles], ACT.Sqrt).then_inc(ln_root, 1)

            def scale(b):
                if b >= B:
                    return
                act.wait_ge(ln_step, LN_STEPS * (1 if b == 0 else 2))
                after(act, xt_full, 2 * (b - 1))
                for t in range(TILES // 2, TILES):
                    last = nc.scalar.activation(xn[:, b % 2, t, :], x_res[:, b * TILES + t, :], ACT.Identity,
                                                bias=small[:, 5, b * TILES + t:b * TILES + t + 1],
                                                scale=small[:, 3, b * TILES + t:b * TILES + t + 1])
                last.then_inc(xn_act, 1)

            def evacuate(b):
                if b >= B:
                    return
                for half in range(2):
                    act.wait_ge(xt_full, 2 * b + half + 1)
                    after(act, v_full, 2 * (b - 1))
                    nc.scalar.activation(xnT[:, b % 2, half * HALF:(half + 1) * HALF], bank[half][:, :],
                                         ACT.Identity, bias=cols[:, 1:2], scale=cols[:, 0:1]).then_inc(xnT_ready, 1)

            def part0(b, n):
                i, half = n // 2, n % 2
                act.wait_ge(qk_full, 4 * b + n + 1)
                after(act, parts_out[b % 2][i], 16 * PARTS * (b // 2))
                nc.scalar.activation(parts[b % 2][i][:, 0, half * HALF:(half + 1) * HALF], qk_ps[n], ACT.Identity,
                                     bias=cols[:, 2 + i:3 + i]).then_inc(part0_done, 1)

            def part1(b, n):
                i, half = n // 2, n % 2
                act.wait_ge(rest_done, 4 * b + n + 1)
                nc.scalar.copy(parts[b % 2][i][:, 1, half * HALF:(half + 1) * HALF], rest[:, n % 2, :]
                               ).then_inc(part1_done, 1)

            act.wait_ge(warm, 1)
            nc.scalar.activation(o_sb[:, 0:TILES], zeros[:], ACT.Sqrt)
            roots(0, 0)
            roots(0, 1)
            scale(0)
            act.wait_ge(consts_in, 16 * N_CONSTS)
            evacuate(0)
            roots(1, 0)
            roots(1, 1)
            scale(1)
            for b in range(B):
                part0(b, 0)
                part0(b, 1)
                part1(b, 0)
                part0(b, 2)
                part1(b, 1)
                part0(b, 3)
                part1(b, 2)
                evacuate(b + 1)
                part1(b, 3)
                scale(b + 2)

            def copy_o(g):
                if not exists(g):
                    return
                act.wait_ge(pv_done, 4 * (g + 1))
                after(act, t_full, g)
                nc.scalar.copy(o_sb[:], o_ps[:, 0:QUARTER]).then_inc(o_copied, 1)

            def head(g, u):
                for c in range(TILES):
                    if c == 2:
                        copy_o(g - 1)
                    after(act, pv_done, 4 * (g - 1) + c // 2 + 1)
                    for half in range(2):
                        n = 2 * c + half
                        act.wait_ge(s2_full, HALVES * g + n + 1)
                        nc.scalar.activation(probs[:, c, half * HALF:(half + 1) * HALF], s2[n % 4][:, :], ACT.Exp,
                                             scale=SCALE).then_inc(exp_done, 1)

            def roots3(part, i):
                tiles = (slice(0, (B - 1) * TILES), slice((B - 1) * TILES, B * TILES))[part]
                act.wait_ge(ln3_step, LN_STEPS * part + 4 * i + 4)
                nc.scalar.activation(small[:, 8 + i, tiles], small[:, 6 + i, tiles], ACT.Sqrt).then_inc(ln3_root, 1)

            over_heads(act, head)
            roots3(0, 0)
            act.wait_ge(bias_turned, 1)
            nc.scalar.copy(b_cols[:], bank[0][:, 0:EXPERTS * (HCH + 1)]).then_inc(b_cols_ready, 1)
            copy_o(HEADS - 1)
            roots3(0, 1)

            def take_rows(n):
                act.wait_ge(rt_full, n + 1)
                after(act, rT_split, n)
                after(act, score_full, n)
                nc.scalar.copy(rT[:, :], t_ps[:, :]).then_inc(rT_ready, 1)
                act.wait_ge(rT_ready, n + 1)
                nc.scalar.copy(rT_high[:, :].rearrange("p (g n) -> p g n", n=GROUP)[:, n, :], rT[:, :]
                               ).then_inc(rT_high_ready, 1)

            def exp_scores(n):
                act.wait_ge(route_step, ROUTE_STEPS * n + 1)
                nc.scalar.activation(route[:, 1, :, :], route[:, 0, :, :], ACT.Exp, scale=-1.0).then_inc(score_exp, 1)

            def take_gates(n):
                act.wait_ge(gt_full, n + 1)
                after(act, gates_out, 16 * n)
                nc.scalar.copy(gT[:, :], t_ps[0:E_ROUTED, :]).then_inc(gT_ready, 1)

            take_rows(0)
            exp_scores(0)

            def up(group, e):
                step = group * EXPERTS + e
                for k in range(HCH + 1):
                    if k == 0 and e == 7 and has_next(group):
                        exp_scores(group + 1)
                    if k < HCH:
                        act.wait_ge(up_full, HCH * step + k + 1)
                        if k == 0:
                            after(act, down_done, step - 1)
                        nc.scalar.activation(hid[:, e % 2, k, :], up_ps[k][:, :], ACT.Gelu,
                                             bias=b_cols[:, e * HCH + k:e * HCH + k + 1]).then_inc(gelu_done, 1)
                    if k > 0:
                        act.wait_ge(gelu_done, HCH * step + k)
                        nc.scalar.copy(hid_high[:, e % 2, k - 1, :], hid[:, e % 2, k - 1, :]).then_inc(high_done, 1)
                    if k == 2 and e == 4 and has_next(group):
                        take_rows(group + 1)
                    if k == 2 and e == 2 and is_first(group):
                        take_gates(0)
                    if k == 0 and e in (5, 6) and is_first(group):
                        roots3(1, e - 5)
                if e == 9 and has_next(group):
                    take_gates(group + 1)

            act.wait_ge(x1_done, B)
            over_groups(act, up)

        @block.vector
        def _(dve):
            V = nc.vector

            def bn(b, done):
                for t in range(b * TILES, (b + 1) * TILES):
                    last = V.bn_stats(stats[:, t, :], x_res[:, t, :])
                last.then_inc(done, 1)

            def norms(tiles, step, count, root, roots, eps, stage):
                s = lambda i: small[:, i, tiles]
                me, m2e, mo, m2o = (stats[:, tiles, i] for i in (1, 2, 4, 5))

                def link(ins, number):
                    ins.then_inc(step, 1)
                    dve.wait_ge(step, count + number)

                if stage == 0:
                    V.tensor_tensor(s(2), me, mo, ALU.add)
                    V.tensor_tensor(s(3), m2e, m2o, ALU.add)
                    link(V.tensor_tensor(s(0), me, mo, ALU.subtract), 1)
                    link(V.scalar_tensor_tensor(s(1), s(0), D / 4.0, s(0), ALU.mult, ALU.mult), 2)
                    link(V.tensor_tensor(s(4), s(3), s(1), ALU.add), 3)
                    link(V.tensor_scalar(s(6), s(4), 1.0 / D, EPS, ALU.mult, ALU.add), 4)
                elif stage == 1:
                    dve.wait_ge(root, roots + 1)
                    link(V.reciprocal(s(10), s(8)), 5)
                    link(V.tensor_tensor(s(0), s(10), s(10), ALU.mult), 6)
                    link(V.scalar_tensor_tensor(s(1), s(4), 1.0 / D, s(0), ALU.mult, ALU.mult), 7)
                    link(V.tensor_scalar(s(7), s(1), 1.0, eps, ALU.mult, ALU.add), 8)
                    V.tensor_scalar(s(1), s(10), 1.0, 1.0, ALU.mult, ALU.add)
                    V.scalar_tensor_tensor(s(0), s(2), -0.5, s(10), ALU.mult, ALU.mult)
                else:
                    dve.wait_ge(root, roots + 2)
                    link(V.reciprocal(s(11), s(9)), 9)
                    link(V.tensor_tensor(s(3), s(10), s(11), ALU.mult), 10)
                    link(V.scalar_tensor_tensor(s(5), s(2), -0.5, s(3), ALU.mult, ALU.mult), 11)

            def scale(b):
                if b >= B:
                    return
                after(dve, xt_full, 2 * (b - 1))
                for t in range(TILES // 2):
                    last = V.tensor_scalar(xn[:, b % 2, t, :], x_res[:, b * TILES + t, :],
                                           small[:, 3, b * TILES + t:b * TILES + t + 1],
                                           small[:, 5, b * TILES + t:b * TILES + t + 1], ALU.mult, ALU.add)
                last.then_inc(xn_dve, 1)

            def remainder(b, n):
                i, half = n // 2, n % 2
                dve.wait_ge(part0_done, 4 * b + n + 1)
                after(dve, parts_ready, 4 * b + n - 1)
                V.scalar_tensor_tensor(rest[:, n % 2, :], qk_ps[n], cols[:, 2 + i:3 + i],
                                       parts[b % 2][i][:, 0, half * HALF:(half + 1) * HALF], ALU.add, ALU.subtract
                                       ).then_inc(rest_done, 1)

            def part2(b, n):
                i, half = n // 2, n % 2
                cs = slice(half * HALF, (half + 1) * HALF)
                dve.wait_ge(part1_done, 4 * b + n + 1)
                V.tensor_tensor(parts[b % 2][i][:, 2, cs], rest[:, n % 2, :], parts[b % 2][i][:, 1, cs], ALU.subtract
                                ).then_inc(parts_ready, 1)

            def take_v(b, half):
                dve.wait_ge(v_full, 2 * b + half + 1)
                shape = [P, TILES // 2, H, DH]
                V.tensor_tensor(v_all[:, b * H:(b + 1) * H, 4 * half:4 * half + 4, :].rearrange("p h t d -> p t h d"),
                                bank[4 + half][:, :].rearrange("p (t h d) -> p t h d", h=H, d=DH),
                                bv_all[:, :].rearrange("p (h d) -> p h d", d=DH).unsqueeze(1).to_broadcast(shape),
                                ALU.add).then_inc(v_ready, 1)

            def norms1(part, stage):
                norms((slice(0, TILES), slice(TILES, B * TILES))[part], ln_step, LN_STEPS * part, ln_root, 2 * part,
                      EPS, stage)

            dve.wait_ge(x_in[0], 16)
            bn(0, bn_done)
            dve.wait_ge(bn_done, 1)
            for stage in range(3):
                norms1(0, stage)
            scale(0)
            for b in range(1, B):
                dve.wait_ge(x_in[b], 16)
                bn(b, bn_done)
            dve.wait_ge(bn_done, B)
            for stage in range(3):
                norms1(1, stage)
            scale(1)
            dve.wait_ge(consts_in, 16 * N_CONSTS)
            for b in range(B):
                remainder(b, 0)
                remainder(b, 1)
                part2(b, 0)
                remainder(b, 2)
                part2(b, 1)
                remainder(b, 3)
                part2(b, 2)
                take_v(b, 0)
                part2(b, 3)
                take_v(b, 1)
                scale(b + 2)

            def half_max(g, u, n):
                if not exists(g):
                    return
                if n == 0:
                    after(dve, split_done, g - 1)
                dve.wait_ge(s1_full, HALVES * g + n + 1)
                nc.vector.tensor_reduce(halfmax[u % 2][:, n:n + 1], s1[ring_bank(g, n)][:, :], AX.X, ALU.max
                                        ).then_inc(half_done, 1)
                if n == HALVES - 1:
                    dve.wait_ge(half_done, HALVES * (g + 1))
                    nc.vector.tensor_reduce(negmax[u % 2][:, :], halfmax[u % 2][:, :].rearrange("p (t s) -> p t s", s=2),
                                            AX.X, ALU.max, negate=True).then_inc(max_done, 1)

            def copy_rows(g, u):
                if not exists(g):
                    return
                dve.wait_ge(mrows_full, g + 1)
                nc.vector.tensor_copy(mrows[u % 2][:], rows_ps).then_inc(mrows_copied, 1)

            def normalise_out(g):
                if not exists(g):
                    return
                dve.wait_ge(t_full, g + 1)
                o = turn_ps.rearrange("p (s j c) -> p s j c", s=2, j=4)
                nc.vector.reciprocal(rsum[:, :, :].unsqueeze(3), o[:, :, :, DH:DH + 1]).then_inc(rsum_done, 1)
                dve.wait_ge(rsum_done, g + 1)
                nc.vector.tensor_tensor(y_all[:, g, :, :].rearrange("p (j s) d -> p s j d", s=2), o[:, :, :, 0:DH],
                                        rsum[:, :, :].unsqueeze(3).to_broadcast([P, 2, 4, DH]), ALU.mult
                                        ).then_inc(norm_done, 1)

            for g in range(2):
                for n in range(HALVES):
                    half_max(g, g, n)
            copy_rows(0, 0)

            def head(g, u):
                for kind, n in RING:
                    if kind == "half":
                        half_max(g + 2, u, n)
                    elif kind == "rows":
                        copy_rows(g + 1, u + 1)
                    else:
                        normalise_out(g - 1)

            x_batches = x_res[:, :, :].rearrange("p (b t) d -> p b t d", b=B)
            y_batches = y_all[:, :, :, :].rearrange("p (b h) t d -> p b t h d", b=B)

            def residual(b):
                dve.wait_ge(norm_done, H * (b + 1))
                xb = x_batches[:, b, :, :].rearrange("p t (h d) -> p t h d", d=DH)
                V.tensor_tensor(xb, xb, y_batches[:, b, :, :, :], ALU.add).then_inc(x1_done, 1)

            def statistics(b):
                dve.wait_ge(x1_done, b + 1)
                bn(b, bn3_done)

            def norms3(part, stage):
                if stage == 0:
                    dve.wait_ge(bn3_done, B - 1 + part)
                norms((slice(0, (B - 1) * TILES), slice((B - 1) * TILES, B * TILES))[part], ln3_step, LN_STEPS * part,
                      ln3_root, 2 * part, EPS_RMS, stage)

            def last_quad(g, u):
                head(g, u)
                if isinstance(g, int) and g == HEADS - 2:
                    for b in range(2):
                        residual(b)
                        statistics(b)
                if isinstance(g, int) and g == HEADS - 1:
                    residual(2)
                    statistics(2)
                    norms3(0, 0)

            over_heads(dve, last_quad)
            norms3(0, 1)
            normalise_out(HEADS - 1)
            norms3(0, 2)
            small_groups = small[:, :, :].rearrange("p i (g t) -> p g i t", g=GROUPS)
            x_groups = x_res[:, :, :].rearrange("p (g t) d -> p g t d", g=GROUPS)

            def scale_rows(n):
                after(dve, rt_full, n)
                wide = [P, GTILES, D]
                factor = lambda i: small_groups[:, n, i, :].unsqueeze(2).to_broadcast(wide)
                xg = x_groups[:, n, :, :]
                V.tensor_tensor(r_tok[:, :, :], xg, factor(3), ALU.mult).then_inc(scale_step, 1)
                V.tensor_tensor(xg, xg, factor(1), ALU.mult).then_inc(scale_step, 1)
                dve.wait_ge(scale_step, 2 * n + 1)
                V.tensor_tensor(r_tok[:, :, :], r_tok[:, :, :], factor(5), ALU.add).then_inc(r_ready, 1)
                dve.wait_ge(scale_step, 2 * n + 2)
                V.tensor_tensor(xg, xg, factor(0), ALU.add).then_inc(x_sum_ready, 1)

            def split_rows(n):
                dve.wait_ge(rT_high_ready, n + 1)
                groups = [r[:, :].rearrange("p (g n) -> p g n", n=GROUP)[:, n, :] for r in (rT_low, rT_high)]
                V.tensor_tensor(groups[0], rT[:, :], groups[1].bitcast(F32), ALU.subtract).then_inc(rT_split, 1)

            rt = lambda i: route[:, i, :, :]

            def take_scores(n):
                dve.wait_ge(score_full, n + 1)
                V.tensor_tensor(rt(0), score_ps, small_groups[:, n, 9, :].unsqueeze(2).to_broadcast([P, GTILES, E_ROUTED]),
                                ALU.mult).then_inc(route_step, 1)

            def gates(n):
                steps = [ROUTE_STEPS * n + 1]

                def rlink(ins):
                    steps[0] = steps[0] + 1
                    ins.then_inc(route_step, 1)
                    dve.wait_ge(route_step, steps[0])

                dve.wait_ge(score_exp, n + 1)
                rlink(V.tensor_scalar(rt(4), rt(1), 1.0, 1.0, ALU.mult, ALU.add))
                rlink(V.reciprocal(rt(3), rt(4)))
                whole = [P, GTILES, E_ROUTED, E_ROUTED]
                s_e = rt(3).unsqueeze(3).to_broadcast(whole)
                s_j = rt(3).unsqueeze(2).to_broadcast(whole)
                flat = lambda i: pairs[:, i, :, :, :]
                V.tensor_tensor(flat(0), s_j, s_e, ALU.is_gt)
                rlink(V.tensor_tensor(flat(1), s_j, s_e, ALU.is_equal))
                rlink(V.tensor_tensor(flat(2), flat(1), before[:, :, :].unsqueeze(1).to_broadcast(whole), ALU.mult))
                rlink(V.tensor_tensor(flat(1), flat(0), flat(2), ALU.add))
                rlink(V.tensor_reduce(rt(4), flat(1), AX.X, ALU.add))
                rlink(V.scalar_tensor_tensor(rt(5), rt(4), float(TOPK), rt(3), ALU.is_lt, ALU.mult))
                rlink(V.tensor_reduce(route[:, 6, :, 0], rt(3), AX.X, ALU.add))
                rlink(V.reciprocal(route[:, 7, :, 0], route[:, 6, :, 0]))
                after(dve, gt_full, n)
                V.tensor_tensor(rt(2), rt(5), route[:, 7, :, 0:1].to_broadcast([P, GTILES, E_ROUTED]), ALU.mult
                                ).then_inc(gates_ready, 1)

            scale_rows(0)
            residual(B - 1)
            dve.wait_ge(b_cols_ready, 1)
            b2 = b_cols[:, EXPERTS * HCH:]
            V.tensor_tensor(b2_shared[:], b2[:, 0:1], b2[:, 1:2], ALU.add)
            split_rows(0)
            take_scores(0)

            def low(group, e):
                step = group * EXPERTS + e
                for k in range(HCH):
                    dve.wait_ge(high_done, HCH * step + k + 1)
                    V.tensor_tensor(hid_low[:, e % 2, k, :], hid[:, e % 2, k, :], hid_high[:, e % 2, k, :].bitcast(F32),
                                    ALU.subtract).then_inc(low_done, 1)
                    if k == 1:
                        gather(group if e > 0 else group - 1, (e - 1) % EXPERTS)
                if e == 1:
                    finish(group - 1)
                if has_next(group):
                    if e == 2:
                        scale_rows(group + 1)
                    elif e == 4:
                        split_rows(group + 1)
                    elif e == 5:
                        take_scores(group + 1)
                    elif e == 7:
                        gates(group + 1)
                if is_first(group):
                    if e == 0:
                        gates(0)
                    elif e == 3:
                        statistics(B - 1)
                        norms3(1, 0)
                    elif e in (5, 6):
                        norms3(1, e - 4)

            def gather(group, e):
                if isinstance(group, int) and group < 0 or e == 0:
                    return
                bank = max(e - E_SHARED + 1, 0) % 3
                dve.wait_ge(down_done, EXPERTS * group + e + 1)
                if e == 1:
                    after(dve, acc_turned, group)
                    V.tensor_scalar(acc[:], y_ps[bank], b2_shared[:, 0:1], 1.0, ALU.add, ALU.mult
                                    ).then_inc(y_read, 1)
                else:
                    r = e - E_SHARED
                    dve.wait_ge(gate_here[r], 16 * (group + 1))
                    after(dve, acc_step, E_ROUTED * group + r)
                    V.scalar_tensor_tensor(gated[:], y_ps[bank], b2[:, e:e + 1], gate_in[:, r, :], ALU.add, ALU.mult
                                           ).then_inc(y_read, 1)

            def finish(group):
                if isinstance(group, int) and group < 0:
                    return
                dve.wait_ge(acc_turned, group + 1)
                dve.wait_ge(x_sum_ready, group + 1)
                xg = x_res[:, :, :].rearrange("p (g t) d -> p g (t d)", g=GROUPS)[:, group, :]
                V.tensor_tensor(xg, t_ps[:, :], xg, ALU.add).then_inc(group_done, 1)

            over_groups(dve, low)
            gather(GROUPS - 1, EXPERTS - 1)
            finish(GROUPS - 1)

        @block.tensor
        def _(pe):
            mm = nc.tensor.matmul

            def turn_x(b):
                if b >= B:
                    return
                pe.wait_ge(xn_dve, b + 1)
                for half in range(2):
                    if half == 1:
                        pe.wait_ge(xn_act, b + 1)
                    after(pe, xnT_ready, 2 * b + half - 1)
                    for tt in range(4):
                        last = nc.tensor.transpose(bank[half][:, tt * P:(tt + 1) * P], xn[:, b % 2, 4 * half + tt, :],
                                                   ident[:])
                    last.then_inc(xt_full, 1)

            def project_qk(b):
                for n in range(4):
                    i, half = n // 2, n % 2
                    if n < 2:
                        pe.wait_ge(xnT_ready, 2 * b + half + 1)
                    after(pe, rest_done, 4 * (b - 1) + n + 1)
                    mm(qk_ps[n], wqkv[:, i, :], xnT[:, b % 2, half * HALF:(half + 1) * HALF],
                       start=True, stop=True).then_inc(qk_full, 1)

            def project_v(b):
                for half in range(2):
                    after(pe, v_ready, 2 * (b - 1) + half + 1)
                    for tt in range(4):
                        t = 4 * half + tt
                        last = mm(bank[4 + half][:, tt * P:(tt + 1) * P], xnT[:, b % 2, t * P:(t + 1) * P],
                                  wqkv[:, 2, :], start=True, stop=True)
                    last.then_inc(v_full, 1)

            pe.wait_ge(ident_ready, 2)
            turn_x(0)
            pe.wait_ge(consts_in, 16 * N_CONSTS)
            for b in range(B):
                project_qk(b)
                turn_x(b + 1)
                project_v(b)

            def bank_free(g, place):
                while True:
                    place -= 3
                    if place < 0 and not (isinstance(g, int) and g <= 0):
                        g, place = g - 1, place + len(RING)
                    last = result(g, place) if place >= 0 else result(-1, place + len(RING))
                    if last is not None:
                        break
                kind, head, n = last
                if kind == "half":
                    pe.wait_ge(half_done, HALVES * head + n + 1)
                elif kind == "rows":
                    pe.wait_ge(mrows_copied, head + 1)
                else:
                    pe.wait_ge(norm_done, head + 1)

            def scores(g, u, n):
                if not exists(g):
                    return
                if n == 0:
                    pe.wait_ge(qk_in[u], 16 * (g - u + SLOTS))
                if not isinstance(g, int) or g >= 2:
                    bank_free(g - 2, RING.index(("half", n)))
                else:
                    after(pe, half_done, HALVES * g + n - 2)
                t, half = n // 2, n % 2
                mm(s1[ring_bank(g, n)][:, :], qs[u][0:STACK, t * P:(t + 1) * P],
                   ks[u][0:STACK, half * HALF:(half + 1) * HALF], start=True, stop=True).then_inc(s1_full, 1)

            def shifted(g, u, n):
                if n == 0:
                    pe.wait_ge(bias_in[u], 4 * (g - u + SLOTS))
                c, half = n // 2, n % 2
                after(pe, exp_done, HALVES * g + n - 3)
                mm(s2[n % 4][:, :], ks[u][:, c * P:(c + 1) * P], qs[u][:, half * HALF:(half + 1) * HALF],
                   start=True, stop=True).then_inc(s2_full, 1)

            def weigh(g, u, c):
                if not exists(g):
                    return
                pe.wait_ge(exp_done, HALVES * g + 2 * c + 2)
                if c == 0:
                    pe.wait_ge(vst_ready, g + 1)
                    after(pe, o_copied, g)
                for j in range(4):
                    last = mm(o_ps[32 * j:32 * j + VCOLS, 0:QUARTER], vst[u % 2][:, c, :],
                              probs[:, c, j * QUARTER:(j + 1) * QUARTER], start=(c == 0), stop=(c == TILES - 1))
                if c % 2 == 1:
                    last.then_inc(pv_done, 1)

            def rows_of_max(g, u):
                if not exists(g):
                    return
                pe.wait_ge(split_done, g + 1)
                if isinstance(g, int) and g == 0:
                    pe.wait_ge(half_done, 2 * HALVES - 2)
                else:
                    bank_free(g - 1, RING.index(("rows", 0)))
                nc.tensor.transpose(rows_ps, mparts[u % 2][:, :, :].rearrange("p i t -> p (i t)"), identb[:]
                                    ).then_inc(mrows_full, 1)

            def turn(g):
                if not exists(g):
                    return
                pe.wait_ge(o_copied, g + 1)
                bank_free(g + 1, RING.index(("turn", 0)))
                for s in range(2):
                    last = nc.tensor.transpose(turn_ps[:, s * P:(s + 1) * P], o_sb[:, s * P:(s + 1) * P], ident[:])
                last.then_inc(t_full, 1)

            pe.wait_ge(rest_done, 4 * B)
            pe.wait_ge(v_ready, 2 * B)
            for g in range(2):
                for n in range(HALVES):
                    scores(g, g, n)
            rows_of_max(0, 0)

            def head(g, u):
                ahead = (u + 2) % SLOTS
                for c in range(TILES):
                    for n in (2 * c, 2 * c + 1):
                        scores(g + 2, ahead, n)
                        shifted(g, u, n)
                    if c == 3:
                        rows_of_max(g + 1, u + 1)
                    if c == 5:
                        turn(g - 1)
                    if c < LAG:
                        weigh(g - 1, u + 1, c + TILES - LAG)
                    else:
                        weigh(g, u, c - LAG)

            over_heads(pe, head)
            pe.wait_ge(ffn_in, 16 * 7)
            pe.wait_ge(max_done, HEADS)
            rows = EXPERTS * (HCH + 1)
            nc.tensor.transpose(bank[0][:, 0:rows], b_rows[:, :], ident[0:rows, 0:rows]).then_inc(bias_turned, 1)
            for c in range(TILES - LAG, TILES):
                weigh(HEADS - 1, HEADS - 1, c)
            turn(HEADS - 1)
            pe.wait_ge(norm_done, HEADS)
            pe.wait_ge(exp_done, HEADS * HALVES)
            pe.wait_ge(b_cols_ready, 1)

            def turn_rows(n):
                pe.wait_ge(r_ready, n + 1)
                for t in range(GTILES):
                    last = nc.tensor.transpose(t_ps[:, t * P:(t + 1) * P], r_tok[:, t, :], ident[:])
                last.then_inc(rt_full, 1)

            def route_rows(n):
                pe.wait_ge(rT_ready, n + 1)
                for t in range(GTILES):
                    last = mm(score_ps[:, t, :], rT[:, t * P:(t + 1) * P], cent[:, :], start=True, stop=True)
                last.then_inc(score_full, 1)

            def turn_gates(n):
                pe.wait_ge(gates_ready, n + 1)
                for t in range(GTILES):
                    last = nc.tensor.transpose(t_ps[0:E_ROUTED, t * P:(t + 1) * P], route[:, 2, t, :], ident[:])
                last.then_inc(gt_full, 1)

            turn_rows(0)
            route_rows(0)

            pe.wait_ge(w_ready, 4)
            rT_high_groups = rT_high[:, :].rearrange("p (g n) -> p g n", g=GROUPS)
            rT_low_groups = rT_low[:, :].rearrange("p (g n) -> p g n", g=GROUPS)

            def step(group, e):
                number = group * EXPERTS + e
                if e == 0:
                    pe.wait_ge(rT_split, group + 1)
                for k in range(HCH):
                    after(pe, gelu_done, HCH * (number - 1) + k + 1)
                    ks_ = slice(k * P, (k + 1) * P)
                    high, low = w1_high[:, e, ks_], w1_low[:, e, ks_]
                    mm(up_ps[k], high, rT_high_groups[:, group, :], start=True, stop=False)
                    mm(up_ps[k], high, rT_low_groups[:, group, :], start=False, stop=False)
                    mm(up_ps[k], low, rT_high_groups[:, group, :], start=False, stop=True).then_inc(up_full, 1)
                if e == 9 and has_next(group):
                    turn_gates(group + 1)
                if e > 0:
                    down(group, e - 1)
                else:
                    down(group - 1, EXPERTS - 1)
                if e == 1:
                    turn_acc(group - 1)
                if e == 1 and is_first(group):
                    turn_gates(0)
                if has_next(group):
                    if e == 3:
                        pe.wait_ge(gT_ready, group + 1)
                        after(pe, group_done, group)
                        turn_rows(group + 1)
                    elif e == 5:
                        route_rows(group + 1)

            def down(group, e):
                if isinstance(group, int) and group < 0:
                    return
                number = group * EXPERTS + e
                index = max(e - E_SHARED + 1, 0)
                result = group * (E_ROUTED + 1) + index
                if e != 1:
                    after(pe, y_read, result - 2)
                for k in range(HCH):
                    pe.wait_ge(low_done, HCH * number + k + 1)
                    high, low = w2_high[:, e, k, :], w2_low[:, e, k, :]
                    first, final = k == 0 and e != 1, k == HCH - 1 and e != 0
                    mm(y_ps[index % 3], high, hid_high[:, e % 2, k, :], start=first, stop=False)
                    mm(y_ps[index % 3], high, hid_low[:, e % 2, k, :], start=False, stop=False)
                    last = mm(y_ps[index % 3], low, hid_high[:, e % 2, k, :], start=False, stop=final)
                last.then_inc(down_done, 1)

            def turn_acc(group):
                if isinstance(group, int) and group < 0:
                    return
                pe.wait_ge(acc_step, E_ROUTED * (group + 1))
                if has_next(group):
                    pe.wait_ge(gT_ready, group + 2)
                else:
                    pe.wait_ge(group_done, group)
                for t in range(GTILES):
                    last = nc.tensor.transpose(t_ps[:, t * P:(t + 1) * P], acc[:, t * P:(t + 1) * P], ident[:])
                last.then_inc(acc_turned, 1)

            over_groups(pe, step)
            down(GROUPS - 1, EXPERTS - 1)
            turn_acc(GROUPS - 1)


def np_size(shape):
    n = 1
    for s in shape:
        n *= s
    return n


_INS = ['L0_attn_x', 'L0_attn_ln_g', 'L0_attn_ln_b', 'L0_attn_Wq', 'L0_attn_bq', 'L0_attn_Wk', 'L0_attn_bk',
        'L0_attn_Wv', 'L0_attn_bv', 'L0_ffn_g_shared', 'L0_ffn_W1_s', 'L0_ffn_b1_s', 'L0_ffn_W2_s', 'L0_ffn_b2_s',
        'L0_ffn_g_routed', 'L0_ffn_W1_r', 'L0_ffn_b1_r', 'L0_ffn_W2_r', 'L0_ffn_b2_r', 'L0_ffn_centroids']


def kernel(**inputs):
    import numpy as _np
    import concourse.bacc as _bacc
    from concourse import mybir as _mybir
    from concourse.bass_utils import run_bass_kernel_spmd as _run

    nc = _bacc.Bacc("TRN2", target_bir_lowering=False, num_devices=1)
    arrays, args = {}, []
    for name in _INS:
        a = _np.ascontiguousarray(inputs[name])
        arrays[f"in_{name}"] = a
        args.append(nc.dram_tensor(f"in_{name}", a.shape, _mybir.dt.from_np(a.dtype), kind="ExternalInput").ap())
    args.append(nc.dram_tensor("out_x", (B, T, D), F32, kind="ExternalOutput").ap())
    transformer_block(nc, *args)
    r = _run(nc, [arrays], core_ids=[0])
    return r.results[0]["out_x"]
```

```python
import math
import struct
from contextlib import ExitStack

import concourse.bass as bass
from concourse import mybir

F32 = mybir.dt.float32
F32R = mybir.dt.float32r
BF16 = mybir.dt.bfloat16
ALU = mybir.AluOpType
ACT = mybir.ActivationFunctionType
AX = mybir.AxisListType

P = 128
B, T, D = 4, 1024, 128
H, DH = 16, 8
TILES = T // P
HALF = 512
EPS = 1e-5
EPS_RMS = 1.1920929e-07
SCALE = 1.0 / math.sqrt(DH)

HEADS = B * H
PARTS = 3
STACK = PARTS * PARTS * DH
BIAS = STACK
TWO_ONES = struct.unpack("f", struct.pack("I", 0x3F803F80))[0]
SLOTS = 4
LAG = 2
VCOLS = 32
DVE_TILES = 2
QUARTER = T // 4

E_SHARED, E_ROUTED, TOPK = 2, 8, 2
EXPERTS = E_SHARED + E_ROUTED
HID = 512
HCH = HID // P
GROUP = 512
GROUPS = B * T // GROUP
GTILES = GROUP // P


def after(eng, sem, count):
    if not isinstance(count, int) or count > 0:
        eng.wait_ge(sem, count)


def over_heads(eng, head):
    for u in range(SLOTS):
        head(u, u)
    with eng.Fori(1, HEADS // SLOTS - 1) as quad:
        for u in range(SLOTS):
            head(quad * SLOTS + u, u)
    for u in range(SLOTS):
        head(HEADS - SLOTS + u, u)


def over_groups(eng, step):
    for e in range(EXPERTS):
        step(0, e)
    with eng.Fori(1, GROUPS - 1) as group:
        for e in range(EXPERTS):
            step(group, e)
    for e in range(EXPERTS):
        step(GROUPS - 1, e)


def has_next(group):
    return not isinstance(group, int) or group < GROUPS - 1


def is_first(group):
    return isinstance(group, int) and group == 0


HALVES = 2 * TILES
EARLY_ROWS = 10

RING = [("half", n) for n in range(8)] + [("rows", 0)] + [("half", n) for n in range(8, 12)] + [("turn", 0)] + \
       [("half", n) for n in range(12, 16)]


def exists(g):
    return not isinstance(g, int) or 0 <= g < HEADS


def result(g, place):
    if isinstance(g, int) and g < 0:
        back = (g * len(RING) + place)
        return ("rows", 0, 0) if back == -1 else ("half", 1, HALVES + back + 1) if back >= -HALVES - 1 else \
            ("half", 0, 2 * HALVES + back + 1)
    kind, n = RING[place]
    head = g + {"half": 2, "rows": 1, "turn": -1}[kind]
    return (kind, head, n) if exists(head) else None


def early_halves(b, i, step):
    if b >= B - 2:
        step(0, 0, HALVES // 2 * (b - (B - 2)) + i)


RING1 = [("turned", 0, 0), ("turned", 0, 1)]
for _b in range(B):
    RING1 += [("qk", _b, n) for n in range(4)]
    RING1 += [("turned", _b + 1, n) for n in range(2) if _b + 1 < B]
    RING1 += [("v", _b, n) for n in range(2)]


def transformer_block(nc, x, ln_g, ln_b, Wq, bq, Wk, bk, Wv, bv, g_shared, W1_s, b1_s, W2_s, b2_s,
                      g_routed, W1_r, b1_r, W2_r, b2_r, centroids, out):
    ctx = ExitStack()
    with ctx:
        top = [nc.sbuf_base + 31 & ~31]

        def sb(name, shape, dt, at=None):
            size = int(np_size(shape[1:])) * (2 if dt == BF16 else 4)
            offset = top[0] if at is None else at
            if at is None:
                top[0] += (size + 31) // 32 * 32
            return nc.alloc_sbuf_tensor_at(name, shape, dt, offset=offset)

        def pb(name, shape=(P, HALF)):
            return ctx.enter_context(nc.psum_tensor(name, list(shape), F32))

        def sem(name):
            return ctx.enter_context(nc.semaphore(name))

        q_scr = nc.dram_tensor("q_scr", (B, H, PARTS, DH, T), BF16, kind="Internal").ap()
        k_scr = nc.dram_tensor("k_scr", (B, H, PARTS, DH, T), BF16, kind="Internal").ap()

        x_res = sb("x_res", [P, B * TILES, D], F32)
        ident = sb("ident", [P, P], F32)
        identb = sb("identb", [P, P], BF16)
        cols = sb("cols", [P, 4], F32)
        base_loop = top[0]
        y_all = sb("y_all", [P, HEADS, TILES, DH], F32)
        v_all = sb("v_all", [P, HEADS, TILES, DH], F32)
        base_slots = top[0]
        qs, ks = [], []
        for i in range(SLOTS):
            qs.append(sb(f"qs{i}", [P, T], BF16))
            ks.append(sb(f"ks{i}", [P, T], BF16))
        base_probs = top[0]
        probs = sb("probs", [P, TILES, T], F32)
        vst = [sb(f"vst{i}", [P, TILES, VCOLS], F32) for i in range(2)]
        negmax = [sb(f"negmax{i}", [P, TILES], F32) for i in range(2)]
        halfmax = [sb(f"halfmax{i}", [P, HALVES], F32) for i in range(2)]
        mparts = [sb(f"mparts{i}", [P, PARTS, TILES], BF16) for i in range(2)]
        zeros = sb("zeros", [P, TILES], F32)
        mrest = sb("mrest", [P, TILES], F32)
        mrows = [sb(f"mrows{i}", [PARTS * TILES, P], BF16) for i in range(2)]
        o_sb = sb("o_sb", [P, QUARTER], F32)
        rsum = sb("rsum", [P, 2, 4], F32)

        w1_high = sb("w1_high", [P, EXPERTS, HID], F32R)
        w1_raw = sb("w1_raw", [P, EXPERTS, HID], F32)
        w1_low = sb("w1_low", [P, EXPERTS, HID], F32R, at=top[0] - EXPERTS * HID * 4)
        w2_high = sb("w2_high", [P, EXPERTS, HCH, D], F32R)
        w2_raw = sb("w2_raw", [P, EXPERTS, HCH, D], F32)
        w2_low = sb("w2_low", [P, EXPERTS, HCH, D], F32R, at=top[0] - EXPERTS * HID * 4)
        g_cols = sb("g_cols", [P, 2], F32)
        b_rows = sb("b_rows", [EXPERTS * (HCH + 1), P], F32)
        b_cols = sb("b_cols", [P, EXPERTS * (HCH + 1)], F32)
        b2_shared = sb("b2_shared", [P, 1], F32)
        cent = sb("cent", [P, E_ROUTED], F32)
        before = sb("before", [P, E_ROUTED, E_ROUTED], F32)
        gates_at = top[0]
        gate_in = sb("gate_in", [P, E_ROUTED, GROUP], F32)
        acc = sb("acc", [P, GROUP], F32)
        gated = sb("gated", [P, GROUP], F32)
        stats = sb("stats", [P, B * TILES, 6], F32)
        small = sb("small", [P, 12, B * TILES], F32)
        pairs = sb("pairs", [P, 3, GTILES, E_ROUTED, E_ROUTED], F32)

        rT_parts = sb("rT_parts", [P, GROUPS, 2, GROUP], F32R, at=base_probs)
        at = base_loop
        hid = sb("hid", [P, 2, HCH, GROUP], F32, at=at)
        hid_low = sb("hid_low", [P, 2, HCH, GROUP], F32R, at=at); at += 2 * HID * 16
        hid_high = sb("hid_high", [P, 2, HCH, GROUP], F32R, at=at); at += 2 * HID * 16
        assert at <= base_slots
        at = base_slots
        r_tok = sb("r_tok", [P, GTILES, D], F32, at=at); at += GTILES * D * 4
        rT = sb("rT", [P, GROUP], F32, at=at); at += GROUP * 4
        gT = sb("gT", [GTILES * E_ROUTED, P], F32, at=at); at += P * 4
        route = sb("route", [P, 8, GTILES, E_ROUTED], F32, at=at); at += 8 * GTILES * E_ROUTED * 4
        assert at <= base_slots + 4 * T * 2

        at = base_probs
        wqkv = sb("wqkv", [P, 3, D], F32, at=at); at += 3 * D * 4
        bv_all = sb("bv_all", [P, D], F32, at=at); at += D * 4
        xn = sb("xn", [P, 2, TILES, D], F32, at=at); at += 2 * TILES * D * 4
        rest01 = sb("rest01", [P, 2, HALF], F32, at=at); at += 2 * HALF * 4
        part_size = PARTS * T * 2
        xnT = sb("xnT", [P, 2, T], F32, at=gates_at)
        parts = [[sb(f"parts{j}{i}", [P, PARTS, T], BF16, at=at + (2 * j + i) * part_size if (j, i) != (1, 1) else
                     gates_at + 2 * T * 4) for i in range(2)] for j in range(2)]
        rest23 = sb("rest23", [P, 2, HALF], F32, at=gates_at + 2 * T * 4 + part_size)
        rest = [rest01[:, 0, :], rest01[:, 1, :], rest23[:, 0, :], rest23[:, 1, :]]
        assert at + 3 * part_size <= base_probs + TILES * T * 4
        assert 2 * T * 4 + part_size + 2 * HALF * 4 <= (E_ROUTED + 2) * GROUP * 4

        gates_scr = nc.dram_tensor("gates_scr", (GROUPS, GTILES * E_ROUTED, P), F32, kind="Internal").ap()

        bank = [pb(f"bank{i}") for i in range(8)]
        s1, s2 = bank[0:3], bank[3:7]

        def ring1(*result):
            return bank[RING1.index(result) % 5][:, :]

        o_ps = bank[7]
        t_ps = bank[7]

        rows_ps = s1[RING.index(("rows", 0)) % 3][0:PARTS * TILES, 0:P // 2].bitcast(BF16)

        def turn_ps(g):
            last = isinstance(g, int) and g == HEADS - 1
            return (o_ps if last else s1[RING.index(("turn", 0)) % 3])[:, 0:2 * P]

        def ring_bank(g, n):
            if isinstance(g, int) and g < 2:
                return 5 + (g * HALVES + n) % 3
            return RING.index(("half", n)) % 3

        up_ps = [b[:, :] for b in bank[0:4]]

        def route_ps(n):
            return bank[0][:, :] if is_first(n) else t_ps[:, :]

        def score_ps(n):
            return route_ps(n)[:, 0:GTILES * E_ROUTED].rearrange("p (t e) -> p t e", e=E_ROUTED)

        y_ps = [b[:, :] for b in bank[4:7]]

        x_batches = x_res[:, :, :].rearrange("p (b t) d -> p b t d", b=B)
        y_batches = y_all[:, :, :, :].rearrange("p (b h) t d -> p b t h d", b=B)

        x_in = [sem(f"x_in{b}") for b in range(B)]
        consts_in = sem("consts_in")
        ident0 = sem("ident0")
        ident_ready = sem("ident_ready")
        pads_ready = sem("pads_ready")
        vst_padded = sem("vst_padded")
        warm = sem("warm")
        bn_done = sem("bn_done")
        ln_step = sem("ln_step")
        ln_root = sem("ln_root")
        xn_dve = sem("xn_dve")
        xn_act = sem("xn_act")
        xt_full = sem("xt_full")
        xnT_ready = sem("xnT_ready")
        qk_full = sem("qk_full")
        part0_done = sem("part0_done")
        rest_done = sem("rest_done")
        part1_done = sem("part1_done")
        parts_ready = sem("parts_ready")
        v_full = sem("v_full")
        v_ready = sem("v_ready")
        parts_out = [[sem(f"parts_out{j}{i}") for i in range(2)] for j in range(2)]

        qk_in = [sem(f"qk_in{i}") for i in range(SLOTS)]
        bias_in = [sem(f"bias_in{i}") for i in range(SLOTS)]
        s1_full = sem("s1_full")
        half_done = sem("half_done")
        max_done = sem("max_done")
        split_step = sem("split_step")
        split_done = sem("split_done")
        mrows_full = sem("mrows_full")
        mrows_copied = sem("mrows_copied")
        s2_full = sem("s2_full")
        exp_done = sem("exp_done")
        vst_ready = sem("vst_ready")
        pv_done = sem("pv_done")
        o_copied = sem("o_copied")
        t_full = sem("t_full")
        rsum_done = sem("rsum_done")
        norm_done = sem("norm_done")
        w_in = [sem(f"w_in{i}") for i in range(4)]
        ffn_in = sem("ffn_in")
        w_split = sem("w_split")
        before_set = sem("before_set")
        before_ready = sem("before_ready")
        bias_turned = sem("bias_turned")
        b_cols_ready = sem("b_cols_ready")
        x1_done = sem("x1_done")
        x1_last = sem("x1_last")
        bn3_done = sem("bn3_done")
        ln3_step = sem("ln3_step")
        ln3_root = sem("ln3_root")
        r_ready = sem("r_ready")
        scale_step = sem("scale_step")
        x_sum_ready = sem("x_sum_ready")
        rt_full = sem("rt_full")
        rT_ready = sem("rT_ready")
        rT_high_ready = sem("rT_high_ready")
        rT_split = sem("rT_split")
        score_full = sem("score_full")
        route_step = sem("route_step")
        score_exp = sem("score_exp")
        gates_ready = sem("gates_ready")
        gt_full = sem("gt_full")
        gT_ready = sem("gT_ready")
        gates_out = sem("gates_out")
        gate_here = [sem(f"gate_here{i}") for i in range(E_ROUTED)]
        up_full = sem("up_full")
        gelu_done = sem("gelu_done")
        high_done = sem("high_done")
        low_done = sem("low_done")
        down_done = sem("down_done")
        y_read = sem("y_read")
        acc_step = sem("acc_step")
        acc_turned = sem("acc_turned")
        group_done = sem("group_done")
        stored = sem("stored")

        block = ctx.enter_context(nc.Block())

        LN_STEPS = 11
        ROUTE_STEPS = 11
        N_CONSTS = 8

        @block.sync
        def _(sp):
            x_tiles = x.rearrange("b (t p) d -> b p t d", p=P)
            sp.dma_start(x_res[:, 0:TILES, :], x_tiles[0]).then_inc(x_in[0], 16)
            for i, v in enumerate((ln_g, ln_b, bq, bk)):
                sp.dma_start(cols[:, i:i + 1], v.rearrange("(p a) -> p a", a=1)).then_inc(consts_in, 16)
            for i, w in enumerate((Wq, Wk, Wv)):
                sp.dma_start(wqkv[:, i, :], w).then_inc(consts_in, 16)
            sp.dma_start(bv_all[:, :], bv.rearrange("(a n) -> a n", a=1).to_broadcast([P, D])
                         ).then_inc(consts_in, 16)
            for b in range(1, B):
                sp.dma_start(x_res[:, b * TILES:(b + 1) * TILES, :], x_tiles[b]).then_inc(x_in[b], 16)

            sp.dma_start(b_rows[0:E_SHARED * HCH, :], b1_s.rearrange("e (k p) -> (e k) p", p=P)).then_inc(ffn_in, 16)
            sp.dma_start(b_rows[E_SHARED * HCH:EXPERTS * HCH, :], b1_r.rearrange("e (k p) -> (e k) p", p=P)
                         ).then_inc(ffn_in, 16)
            sp.dma_start(b_rows[EXPERTS * HCH:EXPERTS * HCH + E_SHARED, :], b2_s).then_inc(ffn_in, 16)
            sp.dma_start(b_rows[EXPERTS * HCH + E_SHARED:, :], b2_r).then_inc(ffn_in, 16)
            sp.dma_start(g_cols[:, 0:1], g_shared.rearrange("(p a) -> p a", a=1)).then_inc(ffn_in, 16)
            sp.dma_start(g_cols[:, 1:2], g_routed.rearrange("(p a) -> p a", a=1)).then_inc(ffn_in, 16)
            sp.dma_start(cent[:, :], centroids).then_inc(ffn_in, 16)
            for i, (w, lo, n) in enumerate(((W1_s, 0, E_SHARED), (W1_r, E_SHARED, E_ROUTED))):
                sp.dma_start(w1_raw[:, lo:lo + n, :], w.rearrange("e p n -> p e n")).then_inc(w_in[i], 16)
            for i, (w, lo, n) in enumerate(((W2_s, 0, E_SHARED), (W2_r, E_SHARED, E_ROUTED))):
                for e in range(n):
                    sp.dma_start(w2_raw[:, lo + e, :, :], w[e].rearrange("(k p) n -> p k n", p=P)
                                 ).then_inc(w_in[2 + i], 16)

            def store_parts(b):
                for i, scr in enumerate((q_scr, k_scr)):
                    sp.wait_ge(parts_ready, 4 * b + 2 * i + 2)
                    for part in range(PARTS):
                        sp.dma_start(scr[b, :, part, :, :], parts[b % 2][i][:, part, :]
                                     ).then_inc(parts_out[b % 2][i], 16)

            q_heads = q_scr.rearrange("b h i d n -> (b h) i d n")
            k_heads = k_scr.rearrange("b h i d n -> (b h) (i d) n")

            def load(g, u):
                if not exists(g):
                    return
                after(sp, s2_full, HALVES * (g - SLOTS + 1))
                for i in range(PARTS):
                    rows = slice(i * PARTS * DH, (i + 1) * PARTS * DH)
                    src = q_heads[g, i, :, :].unsqueeze(0).to_broadcast([PARTS, DH, T])
                    sp.dma_start(qs[u][rows, :], src).then_inc(qk_in[u], 16)
                src = k_heads[g, :, :].unsqueeze(0).to_broadcast([PARTS, PARTS * DH, T])
                sp.dma_start(ks[u][0:STACK, :], src).then_inc(qk_in[u], 16)

            def bias_rows(g, u):
                if not exists(g):
                    return
                sp.wait_ge(mrows_copied, g + 1)
                sp.dma_start(qs[u][BIAS:BIAS + PARTS, :].rearrange("i (t n) -> i t n", n=P),
                             mrows[u % 2][:, :]).then_inc(bias_in[u], 16)

            store_parts(0)
            sp.wait_ge(pads_ready, 1)
            for i in range(2):
                sp.wait_ge(parts_out[0][i], 16 * PARTS)
            for g in range(SLOTS - 1):
                load(g, g)
            for b in range(1, B):
                store_parts(b)
            for i in range(2):
                sp.wait_ge(parts_out[0][i], 16 * PARTS * (B // 2))
                sp.wait_ge(parts_out[1][i], 16 * PARTS * (B // 2))
            bias_rows(0, 0)

            def head(g, u):
                load(g + SLOTS - 1, (u + SLOTS - 1) % SLOTS)
                bias_rows(g + 1, (u + 1) % SLOTS)

            over_heads(sp, head)

            gates_by_expert = gates_scr.rearrange("g (t e) p -> g e t p", e=E_ROUTED)
            out_by_group = out.rearrange("b (g t p) d -> (b g) p t d", p=P, t=GTILES)

            def spread_gates(group):
                sp.wait_ge(gT_ready, group + 1)
                sp.dma_start(gates_scr[group, :, :], gT[:, :]).then_inc(gates_out, 16)
                sp.wait_ge(gates_out, 16 * (group + 1))
                for r in range(E_ROUTED):
                    after(sp, acc_step, E_ROUTED * (group - 1) + r + 1)
                    sp.dma_start(gate_in[:, r, :].rearrange("p (t n) -> p t n", n=P),
                                 gates_by_expert[group, r, :, :].unsqueeze(0).to_broadcast([P, GTILES, P])
                                 ).then_inc(gate_here[r], 16)

            spread_gates(0)
            with sp.Fori(0, GROUPS - 1) as group:
                spread_gates(group + 1)
                sp.wait_ge(group_done, group + 1)
                sp.dma_start(out_by_group[group, :, :, :],
                             x_res[:, :, :].rearrange("p (g t) d -> p g t d", g=GROUPS)[:, group, :, :]
                             ).then_inc(stored, 16)
            sp.wait_ge(group_done, GROUPS)
            sp.dma_start(out_by_group[GROUPS - 1, :, :, :], x_res[:, (GROUPS - 1) * GTILES:, :]).then_inc(stored, 16)
            sp.wait_ge(stored, 16 * GROUPS)

        @block.gpsimd
        def _(pool):
            nc.gpsimd.memset(ident[:], 0.0).then_inc(ident0, 1)
            nc.gpsimd.memset(identb[:], 0.0).then_inc(ident0, 1)
            pool.wait_ge(ident0, 2)
            for m in (ident, identb):
                nc.gpsimd.affine_select(out=m[:], in_=m[:], compare_op=ALU.not_equal, fill=1.0, base=0,
                                        pattern=[[-1, P]], channel_multiplier=1).then_inc(ident_ready, 1)
            nc.gpsimd.memset(zeros[:], 0.0).then_inc(warm, 1)
            for i in range(2):
                nc.gpsimd.memset(vst[i][:, :, DH + 1:], 0.0)
                last = nc.gpsimd.memset(vst[i][:, :, DH:DH + 1], 1.0)
            last.then_inc(vst_padded, 1)
            for u in range(SLOTS):
                nc.gpsimd.memset(qs[u][:, :].bitcast(F32), 0.0)
                last = nc.gpsimd.memset(ks[u][:, :].bitcast(F32), TWO_ONES)
            last.then_inc(pads_ready, 1)

            nc.gpsimd.memset(before[:], 1.0).then_inc(before_set, 1)
            pool.wait_ge(before_set, 1)
            nc.gpsimd.affine_select(out=before[:], in_=before[:], compare_op=ALU.is_gt, fill=0.0, base=0,
                                    pattern=[[1, E_ROUTED], [-1, E_ROUTED]], channel_multiplier=0
                                    ).then_inc(before_ready, 1)

            pool.wait_ge(ffn_in, 16 * 7)
            steps = [0]

            def chain(ins):
                steps[0] += 1
                ins.then_inc(w_split, 1)
                pool.wait_ge(w_split, steps[0])

            def split_w1(lo, n):
                i = 0 if lo < E_SHARED else 1
                raw, high, low = (w[:, lo:lo + n, :] for w in (w1_raw, w1_high, w1_low))
                pool.wait_ge(w_in[i], 16)
                chain(nc.gpsimd.tensor_scalar(high, raw, g_cols[:, i:i + 1], 1.0, ALU.mult, ALU.mult))
                chain(nc.gpsimd.tensor_scalar(raw, raw, g_cols[:, i:i + 1], 1.0, ALU.mult, ALU.mult))
                chain(nc.gpsimd.tensor_tensor(low, raw, high.bitcast(F32), ALU.subtract))

            def split_w2(lo, n):
                raw, high, low = (w[:, lo:lo + n, :, :] for w in (w2_raw, w2_high, w2_low))
                pool.wait_ge(w_in[2], 16 * E_SHARED)
                pool.wait_ge(w_in[3], 16 * E_ROUTED)
                chain(nc.gpsimd.tensor_scalar(high, raw, 1.0, 1.0, ALU.mult, ALU.mult))
                chain(nc.gpsimd.tensor_tensor(low, raw, high.bitcast(F32), ALU.subtract))

            def part2(b, n):
                i, half = n // 2, n % 2
                cs = slice(half * HALF, (half + 1) * HALF)
                pool.wait_ge(part1_done, 4 * b + n + 1)
                nc.gpsimd.tensor_tensor(parts[b % 2][i][:, 2, cs], rest[n], parts[b % 2][i][:, 1, cs], ALU.subtract
                                        ).then_inc(parts_ready, 1)

            split_w1(0, E_SHARED)
            for b in range(B):
                for n in range(4):
                    part2(b, n)
                if b < B - 1:
                    split_w1(E_SHARED + 2 * b, 2)

            def stage_v(g, u):
                if not exists(g):
                    return
                after(pool, pv_done, 4 * (g - 1))
                nc.gpsimd.tensor_copy(vst[u % 2][:, :, 0:DH], v_all[:, g, :, :]).then_inc(vst_ready, 1)

            def split_max(g, u):
                if not exists(g):
                    return
                i = u % 2
                pool.wait_ge(max_done, g + 1)
                after(pool, mrows_full, g - 1)
                nc.gpsimd.tensor_tensor(mparts[i][:, 0, :], negmax[i][:], zeros[:], ALU.add).then_inc(split_step, 1)
                pool.wait_ge(split_step, 3 * g + 1)
                nc.gpsimd.tensor_tensor(mrest[:], negmax[i][:], mparts[i][:, 0, :], ALU.subtract
                                        ).then_inc(split_step, 1)
                pool.wait_ge(split_step, 3 * g + 2)
                nc.gpsimd.tensor_tensor(mparts[i][:, 1, :], mrest[:], zeros[:], ALU.add).then_inc(split_step, 1)
                pool.wait_ge(split_step, 3 * g + 3)
                nc.gpsimd.tensor_tensor(mparts[i][:, 2, :], mrest[:], mparts[i][:, 1, :], ALU.subtract
                                        ).then_inc(split_done, 1)

            pool.wait_ge(v_ready, 2 * B)
            pool.wait_ge(vst_padded, 1)
            stage_v(0, 0)
            split_max(0, 0)
            split_max(1, 1)

            def head(g, u):
                stage_v(g + 1, u + 1)
                split_max(g + 2, u)
                if isinstance(g, int) and g == 0:
                    split_w1(EXPERTS - 2, 2)
                elif isinstance(g, int) and g < 4:
                    split_w2((0, 3, 6)[g - 1], (3, 3, 4)[g - 1])

            def residual(b):
                pool.wait_ge(norm_done, H * (b + 1))
                xb = x_batches[:, b, :, :].rearrange("p t (h d) -> p t h d", d=DH)
                nc.gpsimd.tensor_tensor(xb, xb, y_batches[:, b, :, :, :], ALU.add).then_inc(x1_done, 1)

            def last_quad(g, u):
                if isinstance(g, int) and HEADS - SLOTS <= g < HEADS - 1:
                    residual(g - (HEADS - SLOTS))
                head(g, u)

            over_heads(pool, last_quad)

            def add_result(group, e):
                if e < E_SHARED:
                    return
                pool.wait_ge(y_read, group * (E_ROUTED + 1) + e - E_SHARED + 2)
                nc.gpsimd.tensor_tensor(acc[:], acc[:], gated[:], ALU.add).then_inc(acc_step, 1)

            over_groups(pool, add_result)

        @block.scalar
        def _(act):
            def roots(part, i):
                tiles = (slice(0, TILES), slice(TILES, B * TILES))[part]
                act.wait_ge(ln_step, LN_STEPS * part + 4 * i + 4)
                nc.scalar.activation(small[:, 8 + i, tiles], small[:, 6 + i, tiles], ACT.Sqrt).then_inc(ln_root, 1)

            def scale(b):
                if b >= B:
                    return
                act.wait_ge(ln_step, LN_STEPS * (1 if b == 0 else 2))
                after(act, xt_full, 2 * (b - 1))
                for t in range(DVE_TILES, TILES):
                    last = nc.scalar.activation(xn[:, b % 2, t, :], x_res[:, b * TILES + t, :], ACT.Identity,
                                                bias=small[:, 5, b * TILES + t:b * TILES + t + 1],
                                                scale=small[:, 3, b * TILES + t:b * TILES + t + 1])
                last.then_inc(xn_act, 1)

            def evacuate(b):
                if b >= B:
                    return
                for half in range(2):
                    act.wait_ge(xt_full, 2 * b + half + 1)
                    after(act, v_full, 2 * (b - 1))
                    nc.scalar.activation(xnT[:, b % 2, half * HALF:(half + 1) * HALF], ring1("turned", b, half),
                                         ACT.Identity, bias=cols[:, 1:2], scale=cols[:, 0:1]).then_inc(xnT_ready, 1)

            def part0(b, n):
                i, half = n // 2, n % 2
                act.wait_ge(qk_full, 4 * b + n + 1)
                after(act, parts_out[b % 2][i], 16 * PARTS * (b // 2))
                nc.scalar.activation(parts[b % 2][i][:, 0, half * HALF:(half + 1) * HALF], ring1("qk", b, n),
                                     ACT.Identity, bias=cols[:, 2 + i:3 + i]).then_inc(part0_done, 1)

            def part1(b, n):
                i, half = n // 2, n % 2
                act.wait_ge(rest_done, 4 * b + n + 1)
                nc.scalar.copy(parts[b % 2][i][:, 1, half * HALF:(half + 1) * HALF], rest[n]
                               ).then_inc(part1_done, 1)

            act.wait_ge(warm, 1)
            nc.scalar.activation(o_sb[:, 0:TILES], zeros[:], ACT.Sqrt)
            roots(0, 0)
            roots(0, 1)
            scale(0)
            act.wait_ge(consts_in, 16 * N_CONSTS)
            evacuate(0)
            roots(1, 0)
            roots(1, 1)
            scale(1)
            for b in range(B):
                part0(b, 0)
                part0(b, 1)
                part1(b, 0)
                part0(b, 2)
                part1(b, 1)
                part0(b, 3)
                part1(b, 2)
                evacuate(b + 1)
                part1(b, 3)
                scale(b + 2)

            def copy_o(g):
                if not exists(g):
                    return
                act.wait_ge(pv_done, 4 * (g + 1))
                after(act, t_full, g)
                nc.scalar.copy(o_sb[:], o_ps[:, 0:QUARTER]).then_inc(o_copied, 1)

            def roots3(part, i):
                tiles = (slice(0, TILES), slice(TILES, B * TILES))[part]
                act.wait_ge(ln3_step, LN_STEPS * part + 4 * i + 4)
                nc.scalar.activation(small[:, 8 + i, tiles], small[:, 6 + i, tiles], ACT.Sqrt).then_inc(ln3_root, 1)

            def take_rows(n):
                act.wait_ge(rt_full, n + 1)
                after(act, rT_split, n)
                after(act, score_full, n)
                nc.scalar.copy(rT[:, :], route_ps(n)).then_inc(rT_ready, 1)

            def high_rows(n):
                act.wait_ge(rT_ready, n + 1)
                if is_first(n):
                    act.wait_ge(pv_done, 4 * (HEADS - 1) + 1)
                nc.scalar.copy(rT_parts[:, n, 0, :], rT[:, :]).then_inc(rT_high_ready, 1)

            def exp_scores(n):
                act.wait_ge(route_step, ROUTE_STEPS * n + 1)
                nc.scalar.activation(route[:, 1, :, :], route[:, 0, :, :], ACT.Exp, scale=-1.0).then_inc(score_exp, 1)

            def take_gates(n):
                act.wait_ge(gt_full, n + 1)
                after(act, gates_out, 16 * n)
                nc.scalar.copy(gT[:, :], route_ps(n)[0:GTILES * E_ROUTED, 0:P]).then_inc(gT_ready, 1)

            def head(g, u):
                for c in range(TILES):
                    if c == 2:
                        copy_o(g - 1)
                    first_group(g, c)
                    after(act, pv_done, 4 * (g - 1) + c // 2 + 1)
                    for half in range(2):
                        n = 2 * c + half
                        act.wait_ge(s2_full, HALVES * g + n + 1)
                        nc.scalar.activation(probs[:, c, half * HALF:(half + 1) * HALF], s2[n % 4][:, :], ACT.Exp,
                                             scale=SCALE).then_inc(exp_done, 1)

            def first_group(g, c):
                if not isinstance(g, int):
                    return
                if (g, c) == (HEADS - 3, 4):
                    roots3(0, 0)
                    roots3(0, 1)
                elif (g, c) == (HEADS - 2, 5):
                    take_rows(0)
                elif (g, c) == (HEADS - 1, 1):
                    exp_scores(0)
                elif (g, c) == (HEADS - 1, 4):
                    high_rows(0)

            over_heads(act, head)
            act.wait_ge(bias_turned, 1)
            nc.scalar.copy(b_cols[:], bank[2][:, 0:EXPERTS * (HCH + 1)]).then_inc(b_cols_ready, 1)
            take_gates(0)
            copy_o(HEADS - 1)

            def up(group, e):
                step = group * EXPERTS + e
                for k in range(HCH + 1):
                    if k == 1 and e == 6 and has_next(group):
                        exp_scores(group + 1)
                    if k < HCH:
                        act.wait_ge(up_full, HCH * step + k + 1)
                        if k == 0:
                            after(act, down_done, step - 1)
                        nc.scalar.activation(hid[:, e % 2, k, :], up_ps[k][:, :], ACT.Gelu,
                                             bias=b_cols[:, e * HCH + k:e * HCH + k + 1]).then_inc(gelu_done, 1)
                    if k > 0:
                        act.wait_ge(gelu_done, HCH * step + k)
                        nc.scalar.copy(hid_high[:, e % 2, k - 1, :], hid[:, e % 2, k - 1, :]).then_inc(high_done, 1)
                    if k == 2 and e == 4 and has_next(group):
                        take_rows(group + 1)
                        high_rows(group + 1)
                    if k == 0 and e == 5 and is_first(group):
                        roots3(1, 0)
                        roots3(1, 1)
                if e == 9 and has_next(group):
                    take_gates(group + 1)

            act.wait_ge(x1_done, B - 1)
            act.wait_ge(x1_last, 1)
            over_groups(act, up)

        @block.vector
        def _(dve):
            V = nc.vector

            def bn(b, done):
                for t in range(b * TILES, (b + 1) * TILES):
                    last = V.bn_stats(stats[:, t, :], x_res[:, t, :])
                last.then_inc(done, 1)

            def norms(tiles, step, count, root, roots, eps, stage):
                s = lambda i: small[:, i, tiles]
                me, m2e, mo, m2o = (stats[:, tiles, i] for i in (1, 2, 4, 5))

                def link(ins, number):
                    ins.then_inc(step, 1)
                    dve.wait_ge(step, count + number)

                if stage == 0:
                    V.tensor_tensor(s(2), me, mo, ALU.add)
                    V.tensor_tensor(s(3), m2e, m2o, ALU.add)
                    link(V.tensor_tensor(s(0), me, mo, ALU.subtract), 1)
                    link(V.scalar_tensor_tensor(s(1), s(0), D / 4.0, s(0), ALU.mult, ALU.mult), 2)
                    link(V.tensor_tensor(s(4), s(3), s(1), ALU.add), 3)
                    link(V.tensor_scalar(s(6), s(4), 1.0 / D, EPS, ALU.mult, ALU.add), 4)
                elif stage == 1:
                    dve.wait_ge(root, roots + 1)
                    link(V.reciprocal(s(10), s(8)), 5)
                    link(V.tensor_tensor(s(0), s(10), s(10), ALU.mult), 6)
                    link(V.scalar_tensor_tensor(s(1), s(4), 1.0 / D, s(0), ALU.mult, ALU.mult), 7)
                    link(V.tensor_scalar(s(7), s(1), 1.0, eps, ALU.mult, ALU.add), 8)
                    V.tensor_scalar(s(1), s(10), 1.0, 1.0, ALU.mult, ALU.add)
                    V.scalar_tensor_tensor(s(0), s(2), -0.5, s(10), ALU.mult, ALU.mult)
                else:
                    dve.wait_ge(root, roots + 2)
                    link(V.reciprocal(s(11), s(9)), 9)
                    link(V.tensor_tensor(s(3), s(10), s(11), ALU.mult), 10)
                    link(V.scalar_tensor_tensor(s(5), s(2), -0.5, s(3), ALU.mult, ALU.mult), 11)

            def scale(b):
                if b >= B:
                    return
                after(dve, xt_full, 2 * (b - 1))
                for t in range(DVE_TILES):
                    last = V.tensor_scalar(xn[:, b % 2, t, :], x_res[:, b * TILES + t, :],
                                           small[:, 3, b * TILES + t:b * TILES + t + 1],
                                           small[:, 5, b * TILES + t:b * TILES + t + 1], ALU.mult, ALU.add)
                last.then_inc(xn_dve, 1)

            def remainder(b, n):
                i, half = n // 2, n % 2
                dve.wait_ge(part0_done, 4 * b + n + 1)
                after(dve, parts_ready, 4 * (b - 1) + n + 1)
                V.scalar_tensor_tensor(rest[n], ring1("qk", b, n), cols[:, 2 + i:3 + i],
                                       parts[b % 2][i][:, 0, half * HALF:(half + 1) * HALF], ALU.add, ALU.subtract
                                       ).then_inc(rest_done, 1)

            def take_v(b, half):
                dve.wait_ge(v_full, 2 * b + half + 1)
                shape = [P, TILES // 2, H, DH]
                V.tensor_tensor(v_all[:, b * H:(b + 1) * H, 4 * half:4 * half + 4, :].rearrange("p h t d -> p t h d"),
                                ring1("v", b, half).rearrange("p (t h d) -> p t h d", h=H, d=DH),
                                bv_all[:, :].rearrange("p (h d) -> p h d", d=DH).unsqueeze(1).to_broadcast(shape),
                                ALU.add).then_inc(v_ready, 1)

            def norms1(part, stage):
                norms((slice(0, TILES), slice(TILES, B * TILES))[part], ln_step, LN_STEPS * part, ln_root, 2 * part,
                      EPS, stage)

            dve.wait_ge(x_in[0], 16)
            bn(0, bn_done)
            dve.wait_ge(bn_done, 1)
            for stage in range(3):
                norms1(0, stage)
            scale(0)
            for b in range(1, B):
                dve.wait_ge(x_in[b], 16)
                bn(b, bn_done)
            dve.wait_ge(bn_done, B)
            for stage in range(3):
                norms1(1, stage)
            scale(1)
            dve.wait_ge(consts_in, 16 * N_CONSTS)
            def half_max(g, u, n):
                if not exists(g):
                    return
                if n == 0:
                    after(dve, split_done, g - 1)
                dve.wait_ge(s1_full, HALVES * g + n + 1)
                nc.vector.tensor_reduce(halfmax[u % 2][:, n:n + 1], bank[ring_bank(g, n)][:, :], AX.X, ALU.max
                                        ).then_inc(half_done, 1)
                if n == HALVES - 1:
                    dve.wait_ge(half_done, HALVES * (g + 1))
                    nc.vector.tensor_reduce(negmax[u % 2][:, :], halfmax[u % 2][:, :].rearrange("p (t s) -> p t s", s=2),
                                            AX.X, ALU.max, negate=True).then_inc(max_done, 1)

            for b in range(B):
                remainder(b, 0)
                remainder(b, 1)
                early_halves(b, 0, half_max)
                early_halves(b, 1, half_max)
                remainder(b, 2)
                early_halves(b, 2, half_max)
                remainder(b, 3)
                early_halves(b, 3, half_max)
                take_v(b, 0)
                early_halves(b, 4, half_max)
                early_halves(b, 5, half_max)
                take_v(b, 1)
                scale(b + 2)
                early_halves(b, 6, half_max)
                early_halves(b, 7, half_max)

            def copy_rows(g, u):
                if not exists(g):
                    return
                dve.wait_ge(mrows_full, g + 1)
                nc.vector.tensor_copy(mrows[u % 2][:], rows_ps).then_inc(mrows_copied, 1)

            def normalise_out(g):
                if not exists(g):
                    return
                dve.wait_ge(t_full, g + 1)
                o = turn_ps(g).rearrange("p (s j c) -> p s j c", s=2, j=4)
                nc.vector.reciprocal(rsum[:, :, :].unsqueeze(3), o[:, :, :, DH:DH + 1]).then_inc(rsum_done, 1)
                dve.wait_ge(rsum_done, g + 1)
                nc.vector.tensor_tensor(y_all[:, g, :, :].rearrange("p (j s) d -> p s j d", s=2), o[:, :, :, 0:DH],
                                        rsum[:, :, :].unsqueeze(3).to_broadcast([P, 2, 4, DH]), ALU.mult
                                        ).then_inc(norm_done, 1)

            for n in range(HALVES):
                half_max(1, 1, n)
                if n == EARLY_ROWS:
                    copy_rows(0, 0)

            def ring(g, u):
                for kind, n in RING:
                    if kind == "half":
                        half_max(g + 2, u, n)
                        if isinstance(g, int) and (g, n) == (HEADS - 3, 9):
                            norms3(0, 1)
                    elif kind == "rows":
                        copy_rows(g + 1, u + 1)
                    else:
                        normalise_out(g - 1)


            def statistics(b):
                if b < B - 1:
                    dve.wait_ge(x1_done, b + 1)
                else:
                    dve.wait_ge(x1_last, 1)
                bn(b, bn3_done)

            def norms3(part, stage):
                if stage == 0:
                    dve.wait_ge(bn3_done, (1, B)[part])
                norms((slice(0, TILES), slice(TILES, B * TILES))[part], ln3_step, LN_STEPS * part,
                      ln3_root, 2 * part, EPS_RMS, stage)

            small_groups = small[:, :, :].rearrange("p i (g t) -> p g i t", g=GROUPS)
            x_groups = x_res[:, :, :].rearrange("p (g t) d -> p g t d", g=GROUPS)

            def scale_rows(n, part):
                factor = lambda i: small_groups[:, n, i, :].unsqueeze(2).to_broadcast([P, GTILES, D])
                xg = x_groups[:, n, :, :]
                if part == 0:
                    after(dve, rt_full, n)
                    V.tensor_tensor(r_tok[:, :, :], xg, factor(3), ALU.mult).then_inc(scale_step, 1)
                elif part == 1:
                    dve.wait_ge(scale_step, 2 * n + 1)
                    V.tensor_tensor(r_tok[:, :, :], r_tok[:, :, :], factor(5), ALU.add).then_inc(r_ready, 1)
                elif part == 2:
                    V.tensor_tensor(xg, xg, factor(1), ALU.mult).then_inc(scale_step, 1)
                else:
                    dve.wait_ge(scale_step, 2 * n + 2)
                    V.tensor_tensor(xg, xg, factor(0), ALU.add).then_inc(x_sum_ready, 1)

            def split_rows(n):
                dve.wait_ge(rT_high_ready, n + 1)
                V.tensor_tensor(rT_parts[:, n, 1, :], rT[:, :], rT_parts[:, n, 0, :].bitcast(F32), ALU.subtract
                                ).then_inc(rT_split, 1)

            rt = lambda i: route[:, i, :, :]

            def take_scores(n):
                dve.wait_ge(score_full, n + 1)
                V.tensor_tensor(rt(0), score_ps(n),
                                small_groups[:, n, 9, :].unsqueeze(2).to_broadcast([P, GTILES, E_ROUTED]), ALU.mult).then_inc(route_step, 1)

            def gates(n, part):
                done = lambda i: dve.wait_ge(route_step, ROUTE_STEPS * n + i)
                whole = [P, GTILES, E_ROUTED, E_ROUTED]
                s_e = rt(3).unsqueeze(3).to_broadcast(whole)
                s_j = rt(3).unsqueeze(2).to_broadcast(whole)
                flat = lambda i: pairs[:, i, :, :, :]
                if part == 0:
                    dve.wait_ge(score_exp, n + 1)
                    V.tensor_scalar(rt(4), rt(1), 1.0, 1.0, ALU.mult, ALU.add).then_inc(route_step, 1)
                elif part == 1:
                    done(2)
                    V.reciprocal(rt(3), rt(4)).then_inc(route_step, 1)
                elif part == 2:
                    done(3)
                    V.tensor_tensor(flat(1), s_j, s_e, ALU.is_equal).then_inc(route_step, 1)
                elif part == 3:
                    V.tensor_tensor(flat(0), s_j, s_e, ALU.is_gt).then_inc(route_step, 1)
                elif part == 4:
                    done(5)
                    dve.wait_ge(before_ready, 1)
                    V.tensor_tensor(flat(2), flat(1), before[:, :, :].unsqueeze(1).to_broadcast(whole), ALU.mult
                                    ).then_inc(route_step, 1)
                elif part == 5:
                    done(6)
                    V.tensor_tensor(flat(1), flat(0), flat(2), ALU.add).then_inc(route_step, 1)
                elif part == 6:
                    done(7)
                    V.tensor_reduce(rt(4), flat(1), AX.X, ALU.add).then_inc(route_step, 1)
                    V.tensor_reduce(route[:, 6, :, 0], rt(3), AX.X, ALU.add).then_inc(route_step, 1)
                elif part == 7:
                    done(9)
                    V.scalar_tensor_tensor(rt(5), rt(4), float(TOPK), rt(3), ALU.is_lt, ALU.mult
                                           ).then_inc(route_step, 1)
                    V.reciprocal(route[:, 7, :, 0], route[:, 6, :, 0]).then_inc(route_step, 1)
                else:
                    done(11)
                    after(dve, gt_full, n)
                    V.tensor_tensor(rt(2), rt(5), route[:, 7, :, 0:1].to_broadcast([P, GTILES, E_ROUTED]), ALU.mult
                                    ).then_inc(gates_ready, 1)

            def last_heads(g, u):
                ring(g, u)
                if not isinstance(g, int):
                    return
                if g == HEADS - 4:
                    statistics(0)
                    norms3(0, 0)
                elif g == HEADS - 3:
                    norms3(0, 2)
                    dve.wait_ge(s2_full, HALVES * (HEADS - 2))
                    for part in range(4):
                        scale_rows(0, part)
                elif g == HEADS - 2:
                    statistics(1)
                    statistics(2)
                    take_scores(0)
                    for part in range(9):
                        gates(0, part)
                elif g == HEADS - 1:
                    split_rows(0)

            over_heads(dve, last_heads)
            normalise_out(HEADS - 1)

            dve.wait_ge(norm_done, HEADS)
            xb = x_batches[:, B - 1, :, :].rearrange("p t (h d) -> p t h d", d=DH)
            V.tensor_tensor(xb, xb, y_batches[:, B - 1, :, :, :], ALU.add).then_inc(x1_last, 1)
            dve.wait_ge(b_cols_ready, 1)
            b2 = b_cols[:, EXPERTS * HCH:]
            V.tensor_tensor(b2_shared[:], b2[:, 0:1], b2[:, 1:2], ALU.add)

            def low(group, e):
                step = group * EXPERTS + e
                for k in range(HCH):
                    dve.wait_ge(high_done, HCH * step + k + 1)
                    V.tensor_tensor(hid_low[:, e % 2, k, :], hid[:, e % 2, k, :], hid_high[:, e % 2, k, :].bitcast(F32),
                                    ALU.subtract).then_inc(low_done, 1)
                    if has_next(group):
                        chunk = HCH * e + k
                        if 8 <= chunk < 8 + 4:
                            scale_rows(group + 1, chunk - 8)
                        elif chunk == 19:
                            split_rows(group + 1)
                        elif chunk == 23:
                            take_scores(group + 1)
                        elif 26 <= chunk < 26 + 9:
                            gates(group + 1, chunk - 26)
                    if k == 1:
                        gather(group if e > 0 else group - 1, (e - 1) % EXPERTS)
                if e == 1:
                    finish(group - 1)
                if is_first(group):
                    if e == 3:
                        statistics(B - 1)
                        norms3(1, 0)
                    elif e == 4:
                        norms3(1, 1)
                    elif e == 5:
                        norms3(1, 2)

            def gather(group, e):
                if isinstance(group, int) and group < 0 or e == 0:
                    return
                bank = max(e - E_SHARED + 1, 0) % 3
                dve.wait_ge(down_done, EXPERTS * group + e + 1)
                if e == 1:
                    after(dve, acc_turned, group)
                    V.tensor_scalar(acc[:], y_ps[bank], b2_shared[:, 0:1], 1.0, ALU.add, ALU.mult
                                    ).then_inc(y_read, 1)
                else:
                    r = e - E_SHARED
                    dve.wait_ge(gate_here[r], 16 * (group + 1))
                    after(dve, acc_step, E_ROUTED * group + r)
                    V.scalar_tensor_tensor(gated[:], y_ps[bank], b2[:, e:e + 1], gate_in[:, r, :], ALU.add, ALU.mult
                                           ).then_inc(y_read, 1)

            def finish(group):
                if isinstance(group, int) and group < 0:
                    return
                dve.wait_ge(acc_turned, group + 1)
                dve.wait_ge(x_sum_ready, group + 1)
                xg = x_res[:, :, :].rearrange("p (g t) d -> p g (t d)", g=GROUPS)[:, group, :]
                V.tensor_tensor(xg, t_ps[:, :], xg, ALU.add).then_inc(group_done, 1)

            over_groups(dve, low)
            gather(GROUPS - 1, EXPERTS - 1)
            finish(GROUPS - 1)

        @block.tensor
        def _(pe):
            mm = nc.tensor.matmul

            def bank_free(g, place):
                while True:
                    place -= 3
                    if place < 0 and not (isinstance(g, int) and g <= 0):
                        g, place = g - 1, place + len(RING)
                    last = result(g, place) if place >= 0 else result(-1, place + len(RING))
                    if last is not None:
                        break
                kind, head, n = last
                if kind == "half":
                    pe.wait_ge(half_done, HALVES * head + n + 1)
                elif kind == "rows":
                    pe.wait_ge(mrows_copied, head + 1)
                else:
                    pe.wait_ge(norm_done, head + 1)

            def scores(g, u, n):
                if not exists(g):
                    return
                if n == 0:
                    pe.wait_ge(qk_in[u], 16 * (g - u + SLOTS))
                if not isinstance(g, int) or g >= 2:
                    bank_free(g - 2, RING.index(("half", n)))
                else:
                    after(pe, half_done, HALVES * g + n - 2)
                t, half = n // 2, n % 2
                mm(bank[ring_bank(g, n)][:, :], qs[u][0:STACK, t * P:(t + 1) * P],
                   ks[u][0:STACK, half * HALF:(half + 1) * HALF], start=True, stop=True).then_inc(s1_full, 1)

            def shifted(g, u, n):
                if n == 0:
                    pe.wait_ge(bias_in[u], 4 * (g - u + SLOTS))
                c, half = n // 2, n % 2
                after(pe, exp_done, HALVES * g + n - 3)
                mm(s2[n % 4][:, :], ks[u][:, c * P:(c + 1) * P], qs[u][:, half * HALF:(half + 1) * HALF],
                   start=True, stop=True).then_inc(s2_full, 1)

            def weigh(g, u, c):
                if not exists(g):
                    return
                pe.wait_ge(exp_done, HALVES * g + 2 * c + 2)
                if c == 0:
                    pe.wait_ge(vst_ready, g + 1)
                    after(pe, o_copied, g)
                for j in range(4):
                    last = mm(o_ps[32 * j:32 * j + VCOLS, 0:QUARTER], vst[u % 2][:, c, :],
                              probs[:, c, j * QUARTER:(j + 1) * QUARTER], start=(c == 0), stop=(c == TILES - 1))
                if c % 2 == 1:
                    last.then_inc(pv_done, 1)

            def rows_of_max(g, u):
                if not exists(g):
                    return
                pe.wait_ge(split_done, g + 1)
                if not is_first(g):
                    bank_free(g - 1, RING.index(("rows", 0)))
                nc.tensor.transpose(rows_ps, mparts[u % 2][:, :, :].rearrange("p i t -> p (i t)"), identb[:]
                                    ).then_inc(mrows_full, 1)

            def turn(g):
                if not exists(g):
                    return
                pe.wait_ge(o_copied, g + 1)
                bank_free(g + 1, RING.index(("turn", 0)))
                for s in range(2):
                    last = nc.tensor.transpose(turn_ps(g)[:, s * P:(s + 1) * P], o_sb[:, s * P:(s + 1) * P], ident[:])
                last.then_inc(t_full, 1)

            def ring1_free(*result):
                place = RING1.index(result) - 5
                if place < 0:
                    return
                kind, b, n = RING1[place]
                if kind == "turned":
                    pe.wait_ge(xnT_ready, 2 * b + n + 1)
                elif kind == "qk":
                    pe.wait_ge(rest_done, 4 * b + n + 1)
                else:
                    pe.wait_ge(v_ready, 2 * b + n + 1)

            def turn_x(b):
                if b >= B:
                    return
                pe.wait_ge(xn_dve, b + 1)
                pe.wait_ge(xn_act, b + 1)
                for half in range(2):
                    ring1_free("turned", b, half)
                    for tt in range(4):
                        last = nc.tensor.transpose(ring1("turned", b, half)[:, tt * P:(tt + 1) * P],
                                                   xn[:, b % 2, 4 * half + tt, :], ident[:])
                    last.then_inc(xt_full, 1)

            def project_qk(b, n):
                i, half = n // 2, n % 2
                if n < 2:
                    pe.wait_ge(xnT_ready, 2 * b + half + 1)
                ring1_free("qk", b, n)
                mm(ring1("qk", b, n), wqkv[:, i, :], xnT[:, b % 2, half * HALF:(half + 1) * HALF],
                   start=True, stop=True).then_inc(qk_full, 1)

            def project_v(b, half):
                ring1_free("v", b, half)
                for tt in range(4):
                    t = 4 * half + tt
                    last = mm(ring1("v", b, half)[:, tt * P:(tt + 1) * P], xnT[:, b % 2, t * P:(t + 1) * P],
                              wqkv[:, 2, :], start=True, stop=True)
                last.then_inc(v_full, 1)

            pe.wait_ge(ident_ready, 2)
            turn_x(0)
            pe.wait_ge(consts_in, 16 * N_CONSTS)
            for b in range(B):
                for n in range(4):
                    project_qk(b, n)
                    early_halves(b, n, scores)
                turn_x(b + 1)
                early_halves(b, 4, scores)
                project_v(b, 0)
                early_halves(b, 5, scores)
                project_v(b, 1)
                early_halves(b, 6, scores)
                early_halves(b, 7, scores)

            for n in range(HALVES):
                scores(1, 1, n)
                if n == EARLY_ROWS:
                    pe.wait_ge(rest_done, 4 * B)
                    pe.wait_ge(v_ready, 2 * B)
                    rows_of_max(0, 0)

            def turn_rows(n):
                pe.wait_ge(r_ready, n + 1)
                for t in range(GTILES):
                    last = nc.tensor.transpose(route_ps(n)[:, t * P:(t + 1) * P], r_tok[:, t, :], ident[:])
                last.then_inc(rt_full, 1)

            def route_rows(n):
                pe.wait_ge(rT_ready, n + 1)
                for t in range(GTILES):
                    last = mm(score_ps(n)[:, t, :], rT[:, t * P:(t + 1) * P], cent[:, :], start=True, stop=True)
                last.then_inc(score_full, 1)

            def turn_gates(n):
                pe.wait_ge(gates_ready, n + 1)
                nc.tensor.transpose(route_ps(n)[0:GTILES * E_ROUTED, 0:P],
                                    route[:, 2, :, :].rearrange("p t e -> p (t e)"), ident[:]).then_inc(gt_full, 1)

            def first_group(g, c):
                if not isinstance(g, int):
                    return
                if (g, c) == (HEADS - 2, 3):
                    pe.wait_ge(max_done, HEADS)
                    turn_rows(0)
                elif (g, c) == (HEADS - 2, 7):
                    route_rows(0)
                elif (g, c) == (HEADS - 1, 6):
                    turn_gates(0)

            def head(g, u):
                ahead = (u + 2) % SLOTS
                for c in range(TILES):
                    for n in (2 * c, 2 * c + 1):
                        scores(g + 2, ahead, n)
                        shifted(g, u, n)
                    if c == 3:
                        rows_of_max(g + 1, u + 1)
                    if c == 5:
                        turn(g - 1)
                    first_group(g, c)
                    if c < LAG:
                        weigh(g - 1, u + 1, c + TILES - LAG)
                    else:
                        weigh(g, u, c - LAG)

            over_heads(pe, head)

            pe.wait_ge(ffn_in, 16 * 7)
            pe.wait_ge(mrows_copied, HEADS)
            rows = EXPERTS * (HCH + 1)
            nc.tensor.transpose(bank[2][:, 0:rows], b_rows[:, :], ident[0:rows, 0:rows]).then_inc(bias_turned, 1)
            for c in range(TILES - LAG, TILES):
                weigh(HEADS - 1, HEADS - 1, c)
            turn(HEADS - 1)

            pe.wait_ge(gT_ready, 1)
            pe.wait_ge(norm_done, HEADS - 1)
            pe.wait_ge(b_cols_ready, 1)
            pe.wait_ge(w_split, 3 * EXPERTS // 2 + 2 * 3)

            def step(group, e):
                number = group * EXPERTS + e
                if e == 0:
                    pe.wait_ge(rT_split, group + 1)
                for k in range(HCH):
                    after(pe, gelu_done, HCH * (number - 1) + k + 1)
                    ks_ = slice(k * P, (k + 1) * P)
                    high, low = w1_high[:, e, ks_], w1_low[:, e, ks_]
                    mm(up_ps[k], high, rT_parts[:, group, 0, :], start=True, stop=False)
                    mm(up_ps[k], high, rT_parts[:, group, 1, :], start=False, stop=False)
                    mm(up_ps[k], low, rT_parts[:, group, 0, :], start=False, stop=True).then_inc(up_full, 1)
                if e == 9 and has_next(group):
                    turn_gates(group + 1)
                if e > 0:
                    down(group, e - 1)
                else:
                    down(group - 1, EXPERTS - 1)
                if e == 1:
                    turn_acc(group - 1)
                if has_next(group):
                    if e == 3:
                        if is_first(group):
                            pe.wait_ge(norm_done, HEADS)
                        else:
                            pe.wait_ge(group_done, group)
                        turn_rows(group + 1)
                    elif e == 5:
                        route_rows(group + 1)

            def down(group, e):
                if isinstance(group, int) and group < 0:
                    return
                number = group * EXPERTS + e
                index = max(e - E_SHARED + 1, 0)
                result = group * (E_ROUTED + 1) + index
                if e != 1:
                    after(pe, y_read, result - 2)
                for k in range(HCH):
                    pe.wait_ge(low_done, HCH * number + k + 1)
                    high, low = w2_high[:, e, k, :], w2_low[:, e, k, :]
                    first, final = k == 0 and e != 1, k == HCH - 1 and e != 0
                    mm(y_ps[index % 3], high, hid_high[:, e % 2, k, :], start=first, stop=False)
                    mm(y_ps[index % 3], high, hid_low[:, e % 2, k, :], start=False, stop=False)
                    last = mm(y_ps[index % 3], low, hid_high[:, e % 2, k, :], start=False, stop=final)
                last.then_inc(down_done, 1)

            def turn_acc(group):
                if isinstance(group, int) and group < 0:
                    return
                pe.wait_ge(acc_step, E_ROUTED * (group + 1))
                if has_next(group):
                    pe.wait_ge(gT_ready, group + 2)
                else:
                    pe.wait_ge(group_done, group)
                for t in range(GTILES):
                    last = nc.tensor.transpose(t_ps[:, t * P:(t + 1) * P], acc[:, t * P:(t + 1) * P], ident[:])
                last.then_inc(acc_turned, 1)

            over_groups(pe, step)
            down(GROUPS - 1, EXPERTS - 1)
            turn_acc(GROUPS - 1)


def np_size(shape):
    n = 1
    for s in shape:
        n *= s
    return n


_INS = ['L0_attn_x', 'L0_attn_ln_g', 'L0_attn_ln_b', 'L0_attn_Wq', 'L0_attn_bq', 'L0_attn_Wk', 'L0_attn_bk',
        'L0_attn_Wv', 'L0_attn_bv', 'L0_ffn_g_shared', 'L0_ffn_W1_s', 'L0_ffn_b1_s', 'L0_ffn_W2_s', 'L0_ffn_b2_s',
        'L0_ffn_g_routed', 'L0_ffn_W1_r', 'L0_ffn_b1_r', 'L0_ffn_W2_r', 'L0_ffn_b2_r', 'L0_ffn_centroids']


def kernel(**inputs):
    import numpy as _np
    import concourse.bacc as _bacc
    from concourse import mybir as _mybir
    from concourse.bass_utils import run_bass_kernel_spmd as _run

    nc = _bacc.Bacc("TRN2", target_bir_lowering=False, num_devices=1)
    arrays, args = {}, []
    for name in _INS:
        a = _np.ascontiguousarray(inputs[name])
        arrays[f"in_{name}"] = a
        args.append(nc.dram_tensor(f"in_{name}", a.shape, _mybir.dt.from_np(a.dtype), kind="ExternalInput").ap())
    args.append(nc.dram_tensor("out_x", (B, T, D), F32, kind="ExternalOutput").ap())
    transformer_block(nc, *args)
    r = _run(nc, [arrays], core_ids=[0])
    return r.results[0]["out_x"]
```
